# Optimizing a Trainium2 kernel written in Bass

```python
import numpy as np
import jax
import jax.numpy as jnp

def _softmax(x, axis=-1):
    return jax.nn.softmax(x, axis=axis)

def _gelu(x):
    return jax.nn.gelu(x, approximate=True)

def _silu(x):
    return jax.nn.silu(x)

def _sigmoid(x):
    return jax.nn.sigmoid(x)

def _layernorm(x, axis=-1, eps=1e-05):
    m = jnp.mean(x, axis=axis, keepdims=True)
    v = jnp.var(x, axis=axis, keepdims=True)
    return (x - m) / jnp.sqrt(v + eps)

def _scatter_add(tgt, idx, src, axis=0):
    return tgt.at[idx].add(src)

def _segment_sum(src, seg, n):
    return jax.ops.segment_sum(src, seg, n)
kernel_name = 'mk_adj_preln_d2_adj_r2_3ef8de'

def setup_inputs(seed: int=0):
    np.random.seed(seed)
    _w = jnp.asarray

    def _rec_inputs():
        import jax
        import jax.numpy as jnp
        _gk = jax.random.key(seed)
        x = 7.22e-05 + 1 * jax.random.normal(jax.random.fold_in(_gk, 1), (2048, 512), jnp.float32)
        _a = jax.random.bernoulli(jax.random.fold_in(_gk, 2), 0.000976562, (2048, 2048))
        _a = jnp.logical_or(_a, jnp.swapaxes(_a, -1, -2))
        _a = jnp.logical_or(_a, jnp.eye(2048, dtype=bool))
        _af = _a.astype(jnp.float32)
        _d = jnp.maximum(_af.sum(-1), 1.0) ** (-0.5)
        _af = _af * _d[..., :, None] * _d[..., None, :]
        adj = _af
        return (x, adj)
    x, adj = _rec_inputs()

    def _L0_gnn_setup():
        import jax, jax.numpy as jnp
        import numpy as np
        N = 4096
        D = 512

        def adjacent_mat(adj):
            adj = adj + jnp.eye(adj.shape[0], dtype=adj.dtype)
            deg = jnp.sum(adj, axis=1)
            dinv = jnp.where(deg > 0, deg ** (-0.5), 0.0).astype(adj.dtype)
            return dinv[:, None] * adj * dinv[None, :]
        key = jax.random.key(seed)
        k1, k2 = jax.random.split(key)
        x = jax.random.normal(k1, (N, D), dtype=jnp.float32)
        Coefficient2 = 1e-08 * jnp.ones((N, N), dtype=jnp.float32)
        A = jax.random.uniform(k2, (N, N), dtype=jnp.float32)
        return {'x': x, 'Coefficient2': Coefficient2, 'A': A}
    _L0_gnn_all = _L0_gnn_setup()
    _L0_gnn_in = {k: v for k, v in _L0_gnn_all.items() if k in ()}
    del _L0_gnn_all

    def _L1_gnn_setup():
        import jax, jax.numpy as jnp
        import numpy as np
        import math
        SENT_DIM = 512
        N_SENT = 2048
        key = jax.random.key(seed)
        ks = jax.random.split(key, 8)
        D = SENT_DIM
        s = 1.0 / math.sqrt(D)
        return {'sent_embed': jax.random.normal(ks[0], (N_SENT, D), dtype=jnp.float32), 'adj_tensor': jax.random.randint(ks[1], (N_SENT, N_SENT), 0, 2).astype(jnp.float32), 'W_q': jax.random.uniform(ks[2], (D, D), jnp.float32, -s, s), 'b_q': jax.random.uniform(ks[3], (D,), jnp.float32, -s, s), 'W_k': jax.random.uniform(ks[4], (D, D), jnp.float32, -s, s), 'b_k': jax.random.uniform(ks[5], (D,), jnp.float32, -s, s), 'W_v': jax.random.uniform(ks[6], (D, D), jnp.float32, -s, s), 'b_v': jax.random.uniform(ks[7], (D,), jnp.float32, -s, s)}
    _L1_gnn_all = _L1_gnn_setup()
    _L1_gnn_in = {k: v for k, v in _L1_gnn_all.items() if k in ('W_q', 'b_q', 'W_k', 'b_k', 'W_v', 'b_v')}
    del _L1_gnn_all
    return {'x': x, 'adj': adj, 'L1_gnn_W_q': _L1_gnn_in['W_q'], 'L1_gnn_b_q': _L1_gnn_in['b_q'], 'L1_gnn_W_k': _L1_gnn_in['W_k'], 'L1_gnn_b_k': _L1_gnn_in['b_k'], 'L1_gnn_W_v': _L1_gnn_in['W_v'], 'L1_gnn_b_v': _L1_gnn_in['b_v']}

def reference(x, adj, L1_gnn_W_q, L1_gnn_b_q, L1_gnn_W_k, L1_gnn_b_k, L1_gnn_W_v, L1_gnn_b_v):
    import jax
    import jax.numpy as jnp

    def _L0_gnn_ref(x, Coefficient2, A):
        import jax, jax.numpy as jnp
        import numpy as np
        N = 4096
        D = 512

        def adjacent_mat(adj):
            adj = adj + jnp.eye(adj.shape[0], dtype=adj.dtype)
            deg = jnp.sum(adj, axis=1)
            dinv = jnp.where(deg > 0, deg ** (-0.5), 0.0).astype(adj.dtype)
            return dinv[:, None] * adj * dinv[None, :]
        A_c = jax.lax.stop_gradient(A)
        adj = adjacent_mat((A_c + A_c.T) * 0.5)
        y = Coefficient2 @ adj
        y = y @ x
        return y

    def _L1_gnn_ref(sent_embed, adj_tensor, W_q, b_q, W_k, b_k, W_v, b_v):
        import jax, jax.numpy as jnp
        import numpy as np
        import math
        SENT_DIM = 512
        N_SENT = 2048
        q = sent_embed @ W_q.T + b_q
        k = sent_embed @ W_k.T + b_k
        v = sent_embed @ W_v.T + b_v
        scale = 1.0 / math.sqrt(sent_embed.shape[-1])
        z = scale * (q @ k.T)
        spare_z = z * adj_tensor
        spare_z = jnp.where(spare_z == 0.0, jnp.asarray(-10000.0, spare_z.dtype), spare_z)
        attn = jax.nn.softmax(spare_z, axis=1)
        out = attn @ v
        return jax.nn.relu(out)
    h = jnp.maximum(_layernorm(x, axis=-1), 0.0)
    x = x + _L0_gnn_ref(h, adj, adj)
    h = jnp.maximum(_layernorm(x, axis=-1), 0.0)
    x = x + _L1_gnn_ref(h, adj, L1_gnn_W_q, L1_gnn_b_q, L1_gnn_W_k, L1_gnn_b_k, L1_gnn_W_v, L1_gnn_b_v)
    return x

_drawn_inputs = setup_inputs


def setup_inputs(seed=0):
    import zlib

    import numpy as np

    out = dict(_drawn_inputs(seed))
    spreads = {}
    factors = {'L1_gnn_W_q': 8.0,
     'L1_gnn_b_q': 64.0,
     'L1_gnn_W_k': 8.0,
     'L1_gnn_b_k': 200.0,
     'L1_gnn_b_v': 4.078}
    for name, (base, spread) in spreads.items():
        noise = np.random.default_rng([zlib.crc32(name.encode()), seed]).standard_normal(out[name].shape)
        drawn = base * np.exp(spread * noise) if base else spread * noise
        out[name] = jnp.asarray(drawn.astype(out[name].dtype))
    for name, factor in factors.items():
        out[name] = (out[name] * factor).astype(out[name].dtype)
    return out
```

```python
import concourse.bass as bass
from concourse import mybir
from concourse.alu_op_type import AluOpType as ALU
from contextlib import ExitStack

N = 2048
D = 512
P = 128
NT = N // P
DT = D // P
QT = 4
NQ = NT // QT
EPS = 1e-5
MASKED = -10000.0
SCALE = 1.0 / float(D) ** 0.5
TINY = 1.17549435e-38


def build(nc, x, adj, w_q, b_q, w_k, b_k, w_v, b_v, out):
    f32, f32r = mybir.dt.float32, mybir.dt.float32r
    ACT = mybir.ActivationFunctionType
    AX = mybir.AxisListType.X
    ds = bass.ds

    x_t = x.rearrange("(t p) d -> p t d", p=P)
    wq_t = w_q.rearrange("(t p) d -> p t d", p=P)
    wk_t = w_k.rearrange("(t p) d -> p t d", p=P)
    wv_t = w_v.rearrange("(t p) d -> p t d", p=P)
    x1_dram = nc.dram_tensor("x1_scratch", [N, D], f32).ap()

    BASE = (nc.sbuf_base + 31) // 32 * 32
    KB = 1024
    REG_S = BASE
    REG_G = REG_S + 128 * KB
    REG_R = REG_G + 64 * KB

    def at(name, shape, dt, offset):
        return nc.alloc_sbuf_tensor_at(name, shape, dt, offset=offset)

    S = at("S", [P, NT, N], f32, REG_S)
    U = at("U", [P, NT // 2, N], f32r, REG_S)
    W = at("W", [P, NT // 2, N], f32, REG_S + 64 * KB)
    HT = at("HT", [P, 2 * DT, N], f32r, REG_S + 64 * KB)
    V = at("V", [P, 2, NT, D], f32r, REG_S)
    H0 = at("H0", [P, NT, D], f32, REG_G + 32 * KB)
    G_hi = at("G_hi", [P, NT, D], f32r, REG_G)
    G_lo = at("G_lo", [P, NT, D], f32r, REG_G + 32 * KB)
    A_row = at("A_row", [P, 2, N], f32, REG_G)
    M_w = at("M_w", [P, 2, DT, D], f32r, REG_G + 16 * KB)
    WvT = at("WvT", [P, 2, DT, D], f32r, REG_G + 32 * KB)
    x_in = at("x_in", [P, 2, D], f32, REG_G + 48 * KB)
    x_out = at("x_out", [P, 2, D], f32, REG_G + 52 * KB)
    normed = at("normed", [P, 2, D], f32, REG_G + 56 * KB)
    adj_row = at("adj_row", [P, N], f32, REG_G)
    prob = [at("prob0", [P, N], f32, REG_G + 8 * KB), at("prob1", [P, N], f32, REG_G + 56 * KB)]
    QT_ = at("QT", [P, 2, DT, D], f32r, REG_G + 32 * KB)
    ring_hi = [at(f"ring_hi{b}", [P, QT, P], f32r, REG_R + 2 * KB * b) for b in range(2)]
    ring_lo = [at(f"ring_lo{b}", [P, QT, P], f32r, REG_R + 4 * KB + 2 * KB * b) for b in range(2)]
    PARTS = NQ + NT
    row_parts = at("row_parts", [P, NT, PARTS], f32, REG_R)
    junk0 = at("junk0", [P, P], f32, REG_R + 2 * KB)
    bn0 = at("bn0", [P, NT, 6], f32, REG_R + 3 * KB)
    mv0 = at("mv0", [P, NT, 2], f32, REG_R + 4 * KB)
    ident = at("ident", [P, P], f32, REG_R + 8 * KB)
    wrow = at("wrow", [P, D], f32, REG_R + 8 * KB + 512)
    bv_row = at("bv_row", [P, D], f32, REG_R + 10 * KB + 512)
    junk = at("junk", [P, D], f32, REG_R + 12 * KB + 512)
    small = REG_R + 14 * KB + 512
    cols = {}
    for name, n in (("neg_half", NT), ("deg", NT), ("deg_pos", NT), ("dinv", NT), ("half_dinv", NT),
                    ("rstd0", NT), ("shift0", NT), ("cbias", NT), ("bq_col", DT), ("bk_col", DT),
                    ("qbias", DT), ("c0", 1), ("bn", 12), ("mv", 4), ("vareps", 2), ("rstd", 2),
                    ("mx4", 8), ("nmax", 2), ("rowsum", 2), ("rinv", 2)):
        cols[name] = at(name, [P, n], f32, small)
        small += (4 * n + 31) // 32 * 32
    assert small <= nc.sbuf_usable_end, (small, nc.sbuf_usable_end)
    neg_half, deg, deg_pos, dinv, half_dinv = (cols[k] for k in ("neg_half", "deg", "deg_pos", "dinv", "half_dinv"))
    rstd0, shift0, cbias, bq_col, bk_col = (cols[k] for k in ("rstd0", "shift0", "cbias", "bq_col", "bk_col"))
    qbias, c0, bn, mv, vareps, rstd = (cols[k] for k in ("qbias", "c0", "bn", "mv", "vareps", "rstd"))
    mx4, nmax, rowsum, rinv = (cols[k] for k in ("mx4", "nmax", "rowsum", "rinv"))

    def w_view(n):
        return W[:, 2 * n:2 * n + 2, 0:2 * D]

    def w_tile(n, t):
        return W[:, 2 * n + t // 2, (t % 2) * D:(t % 2 + 1) * D]

    def bk_rep(t):
        return W[:, 6, t * P:(t + 1) * P]

    ctx = ExitStack()
    with ctx:
        bank = [ctx.enter_context(nc.psum_tensor(f"bank{i}", [P, D], f32)) for i in range(8)]
        Z, TB, Y = bank[0:4], bank[4:6], bank[6:8]

        def sem(name):
            return ctx.enter_context(nc.semaphore(name))

        a_in = [sem(f"a_in{r}") for r in range(NT)]
        x_all_in = sem("x_all_in")
        bias_in = sem("bias_in")
        w_in = sem("w_in")
        arow_in = [sem(f"arow_in{i}") for i in range(2)]
        xt_in = [sem(f"xt_in{i}") for i in range(2)]
        x1_stored = [sem(f"x1_stored{i}") for i in range(2)]
        adj_in = sem("adj_in")
        x1_in = [sem(f"x1_in{i}") for i in range(2)]
        out_stored = [sem(f"out_stored{i}") for i in range(2)]
        ident_step, ident_ready, half_ready = sem("ident_step"), sem("ident_ready"), sem("half_ready")
        t0_done, s_added, parts_act = sem("t0_done"), sem("s_added"), sem("parts_act")
        diag_ready = sem("diag_ready")
        bn0_ready, mv0_ready, var0_ready, rstd0_ready, shift0_ready = (
            sem(k) for k in ("bn0_ready", "mv0_ready", "var0_ready", "rstd0_ready", "shift0_ready"))
        h0_ready, deg_step, dpow_ready, dinv_ready, hdinv_ready = (
            sem(k) for k in ("h0_ready", "deg_step", "dpow_ready", "dinv_ready", "hdinv_ready"))
        g_hi_ready, g_ready = sem("g_hi_ready"), sem("g_ready")
        hi_ready, lo_ready, ring_used = sem("hi_ready"), sem("lo_ready"), sem("ring_used")
        blocks_T = sem("blocks_T")
        u_hi_ready, u_ready = sem("u_hi_ready"), sem("u_ready")
        bk_rep_ready, wsmall_done, wsmall_ready = sem("bk_rep_ready"), sem("wsmall_done"), sem("wsmall_ready")
        wprod_done, wprod_hi, wprod_lo = sem("wprod_done"), sem("wprod_hi"), sem("wprod_lo")
        x1_ready, bn_ready, mv_ready, var_ready, rstd_ready, norm_ready = (
            sem(k) for k in ("x1_ready", "bn_ready", "mv_ready", "var_ready", "rstd_ready", "norm_ready"))
        cdot_ready, cbias_ready = sem("cdot_ready"), sem("cbias_ready")
        h_T, hT_hi, hT_lo = sem("h_T"), sem("hT_hi"), sem("hT_lo")
        v_done = sem("v_done")
        vsum_ready, v_hi_ready, v_ready = sem("vsum_ready"), sem("v_hi_ready"), sem("v_ready")
        qt_done, qt_hi, qt_lo = sem("qt_done"), sem("qt_hi"), sem("qt_lo")
        z_done, s_ready, mask_ready, masked_ready = sem("z_done"), sem("s_ready"), sem("mask_ready"), sem("masked_ready")
        rmax_ready, nmax_ready, prob_ready = sem("rmax_ready"), sem("nmax_ready"), sem("prob_ready")
        rinv_ready, relu_ready, out_ready = sem("rinv_ready"), sem("relu_ready"), sem("out_ready")

        RING2, RING3 = NT * NQ, 2 * NT * NQ

        def batches(r):
            return [(c, min(c + QT, r + 1)) for c in range(0, r + 1, QT)]

        STEPS0 = [(r, b, c0_, c1_) for r in range(NT) for b, (c0_, c1_) in enumerate(batches(r))]

        def below(r, c1_):
            return min(c1_, r)

        ACT_SUMS = 12

        def three(pe_out, hi_l, lo_l, hi_r, lo_r, first, last):
            nc.tensor.matmul(pe_out, hi_l, hi_r, start=first, stop=False)
            nc.tensor.matmul(pe_out, hi_l, lo_r, start=False, stop=False)
            return nc.tensor.matmul(pe_out, lo_l, hi_r, start=False, stop=last)

        block = ctx.enter_context(nc.Block())

        @block.sync
        def _(sp):
            for r in range(NT):
                sp.dma_start(S[:, r, :], adj[r * P:(r + 1) * P, :]).then_inc(a_in[r], 16)
                if r < 4:
                    sp.dma_start(H0[:, 4 * r:4 * r + 4, :], x_t[:, 4 * r:4 * r + 4, :]).then_inc(x_all_in, 16)
            with nc.allow_non_contiguous_dma(reason="512 bias values, one a partition and tile"):
                sp.dma_start(bq_col[:, :], b_q.rearrange("(t p) -> p t", p=P)).then_inc(bias_in, 16)
                sp.dma_start(bk_col[:, :], b_k.rearrange("(t p) -> p t", p=P)).then_inc(bias_in, 16)
            sp.dma_start(bv_row[:, :], b_v.partition_broadcast(P)).then_inc(bias_in, 16)
            sp.wait_ge(lo_ready, NT // 2 * NQ)
            for n, w_dram in enumerate((wq_t, wk_t, wv_t)):
                for h in range(2):
                    sp.dma_start(W[:, 2 * n + h, 0:2 * D].rearrange("p (t d) -> p t d", t=2),
                                 w_dram[:, 2 * h:2 * h + 2, :]).then_inc(w_in, 16)
            sp.wait_ge(ring_used, RING2)

            def rows_in(m, j):
                sp.dma_start(A_row[:, j, :], adj[ds(m * P, P), :]).then_inc(arow_in[j], 16)
                sp.dma_start(x_in[:, j, :], x[ds(m * P, P), :]).then_inc(xt_in[j], 16)

            def x1_store(m, j):
                sp.wait_ge(x1_ready, m + 1)
                sp.dma_start(x1_dram[ds(m * P, P), :], x_out[:, j, :]).then_inc(x1_stored[j], 16)

            for m in range(2):
                rows_in(m, m)
            with sp.Fori(0, NT // 2 - 1) as i:
                for j in range(2):
                    m = 2 * i + j
                    sp.wait_ge(x1_ready, m + 1)
                    sp.wait_ge(blocks_T, NQ * m + NQ)
                    rows_in(m + 2, j)
                    x1_store(m, j)
            for m in range(NT - 2, NT):
                x1_store(m, m % 2)
            for j in range(2):
                sp.wait_ge(x1_stored[j], 16 * NT // 2)

            def phase3_in(i, j):
                sp.dma_start(x_in[:, j, :], x1_dram[ds(i * P, P), :]).then_inc(x1_in[j], 16)
                sp.dma_start(adj_row[:, :], adj[ds(i * P, P), :]).then_inc(adj_in, 16)

            def out_store(i, j):
                sp.wait_ge(out_ready, i + 1)
                sp.dma_start(out[ds(i * P, P), :], x_out[:, j, :]).then_inc(out_stored[j], 16)

            phase3_in(0, 0)
            sp.wait_ge(s_ready, NQ)
            phase3_in(1, 1)
            with sp.Fori(0, NT // 2 - 1) as i:
                for j in range(2):
                    t = 2 * i + j
                    out_store(t, j)
                    sp.wait_ge(s_ready, NQ * t + 2 * NQ)
                    phase3_in(t + 2, j)
            for t in range(NT - 2, NT):
                out_store(t, t % 2)
            for j in range(2):
                sp.wait_ge(out_stored[j], 16 * NT // 2)

        @block.tensor
        def _(pe):
            pe.wait_ge(ident_ready, 1)
            for n, (r, b, c0_, c1_) in enumerate(STEPS0):
                if b == 0:
                    pe.wait_ge(a_in[r], 16)
                if n >= 4:
                    pe.wait_ge(s_added, n - 3)
                up, low = bank[2 * (n % 4)], bank[2 * (n % 4) + 1]
                for c in range(c0_, below(r, c1_)):
                    nc.tensor.transpose(up[:, (c - c0_) * P:(c - c0_ + 1) * P], S[:, r, c * P:(c + 1) * P], ident[:, :])
                for c in range(c0_, c1_):
                    last = nc.tensor.transpose(low[:, (c - c0_) * P:(c - c0_ + 1) * P],
                                               S[:, c, r * P:(r + 1) * P], ident[:, :])
                last.then_inc(t0_done, 1)
            pe.wait_ge(s_added, len(STEPS0))

            def phase1(m, j):
                if not isinstance(m, int) or m >= 2:
                    pe.wait_ge(u_ready, m - 1)
                for q in range(NQ):
                    pe.wait_ge(lo_ready, NQ * m + q + 1)
                    for k in range(QT):
                        t = QT * q + k
                        if isinstance(m, int) and m == 0:
                            pe.wait_ge(g_ready, t + 1)
                        last = three(Y[j][:, :], ring_hi[q % 2][:, k, :], ring_lo[q % 2][:, k, :],
                                     G_hi[:, t, :], G_lo[:, t, :], t == 0, t == NT - 1)
                    last.then_inc(ring_used, 1)

            for m in range(2):
                phase1(m, m)
            with pe.Fori(1, NT // 2) as i:
                for j in range(2):
                    phase1(2 * i + j, j)

            pe.wait_ge(w_in, 16 * 6)
            pe.wait_ge(bk_rep_ready, DT)
            for a in range(DT):
                for e in range(DT):
                    nc.tensor.matmul(TB[0][:, a:a + 1], w_tile(1, e)[:, a * P:(a + 1) * P], bq_col[:, e:e + 1],
                                     start=(e == 0), stop=(e == DT - 1))
            for e in range(DT):
                nc.tensor.matmul(TB[0][:, DT:DT + 1], bk_rep(e), bq_col[:, e:e + 1], start=(e == 0), stop=(e == DT - 1))
            for e in range(DT):
                last = nc.tensor.matmul(TB[1][:, :], bk_rep(e), w_tile(0, e), start=(e == 0), stop=(e == DT - 1))
            last.then_inc(wsmall_done, 1)
            for a in range(DT):
                for e in range(DT):
                    last = nc.tensor.matmul(Z[a][:, :], w_tile(0, e)[:, a * P:(a + 1) * P], w_tile(1, e),
                                            start=(e == 0), stop=(e == DT - 1))
                last.then_inc(wprod_done, 1)
            for a in range(DT):
                pe.wait_ge(wprod_lo, a + 1)
                for e in range(DT):
                    last = nc.tensor.transpose(Z[a][:, e * P:(e + 1) * P], w_tile(2, e)[:, a * P:(a + 1) * P], ident[:, :])
                last.then_inc(wprod_done, 1)

            def transposes(q, j):
                for k in range(QT):
                    last = nc.tensor.transpose(TB[q % 2][:, k * P:(k + 1) * P],
                                               A_row[:, j, (QT * q + k) * P:(QT * q + k + 1) * P], ident[:, :])
                last.then_inc(blocks_T, 1)

            def transpose_h(m, j):
                pe.wait_ge(norm_ready, m + 1)
                if not isinstance(m, int) or m >= 2:
                    pe.wait_ge(hT_lo, m - 1)
                else:
                    pe.wait_ge(wprod_lo, 2 * DT)
                for a in range(DT):
                    last = nc.tensor.transpose(Z[j][:, a * P:(a + 1) * P], normed[:, j, a * P:(a + 1) * P], ident[:, :])
                last.then_inc(h_T, 1)

            def phase2(m, j):
                if not isinstance(m, int) or m >= 2:
                    pe.wait_ge(x1_ready, m - 1)
                for q in range(NQ):
                    if q < NQ - 1:
                        transposes(q + 1, j)
                    elif not isinstance(m, int) or m < NT - 1:
                        pe.wait_ge(arow_in[1 - j], arrived(m, j))
                        transposes(0, 1 - j)
                    if q == 2 and (not isinstance(m, int) or m >= 1):
                        transpose_h(m - 1, 1 - j)
                    pe.wait_ge(lo_ready, NQ * m + RING2 + q + 1)
                    for k in range(QT):
                        t = QT * q + k
                        u = U[:, :, t * P:(t + 1) * P]
                        last = three(Y[j][:, :].rearrange("p (c n) -> p c n", c=QT), ring_hi[q % 2][:, k, :], ring_lo[q % 2][:, k, :],
                                     u[:, 0:QT, :], u[:, QT:2 * QT, :], t == 0, t == NT - 1)
                    last.then_inc(ring_used, 1)

            def arrived(m, j):
                return 16 * ((m + 1) // 2 + 1) if isinstance(m, int) else 8 * (m - j) + 16 * j + 16

            pe.wait_ge(wsmall_ready, 2)
            pe.wait_ge(arow_in[0], 16)
            transposes(0, 0)
            pe.wait_ge(u_ready, NT)
            for m in range(2):
                phase2(m, m)
            with pe.Fori(1, NT // 2 - 1) as i:
                for j in range(2):
                    phase2(2 * i + j, j)
            for m in range(NT - 2, NT):
                phase2(m, m % 2)

            def v_tile(t):
                pe.wait_ge(hT_lo, t + 1)
                if t < 2:
                    pe.wait_ge(x1_ready, NT - 1 + t)
                else:
                    pe.wait_ge(vsum_ready, t - 1)
                for a in range(DT):
                    rows = slice(t * P, (t + 1) * P)
                    last = three(Y[t % 2][:, :], HT[:, a, rows], HT[:, DT + a, rows],
                                 WvT[:, 0, a, :], WvT[:, 1, a, :], a == 0, a == DT - 1)
                last.then_inc(v_done, 1)

            for t in range(NT):
                if t == 2:
                    transpose_h(NT - 1, 1)
                v_tile(t)

            def q_group(g):
                for a in range(DT):
                    if a >= 2:
                        pe.wait_ge(qt_lo, DT * g + a - 1)
                    for d in range(DT):
                        cols_g = ds(g * D, D)
                        last = three(TB[a % 2][:, :], M_w[:, 0, d, a * P:(a + 1) * P], M_w[:, 1, d, a * P:(a + 1) * P],
                                     HT[:, d, cols_g], HT[:, DT + d, cols_g], d == 0, d == DT - 1)
                    last.then_inc(qt_done, 1)

            def z_bank(t, r, n):
                pe.wait_ge(s_ready, NQ * t + n - (NQ - 1)) if not isinstance(t, int) or t >= 1 else None
                for d in range(DT):
                    last = three(Z[n][:, :], QT_[:, 0, d, r * P:(r + 1) * P], QT_[:, 1, d, r * P:(r + 1) * P],
                                 HT[:, d, n * D:(n + 1) * D], HT[:, DT + d, n * D:(n + 1) * D], d == 0, d == DT - 1)
                last.then_inc(z_done, 1)

            def transpose_p(j, q):
                for k in range(QT):
                    last = nc.tensor.transpose(TB[q % 2][:, k * P:(k + 1) * P],
                                               prob[j][:, (QT * q + k) * P:(QT * q + k + 1) * P], ident[:, :])
                last.then_inc(blocks_T, 1)

            def pv(t, j, q):
                pe.wait_ge(lo_ready, NQ * t + RING3 + q + 1)
                for k in range(QT):
                    c = QT * q + k
                    last = three(Y[j][:, :], ring_hi[q % 2][:, k, :], ring_lo[q % 2][:, k, :],
                                 V[:, 0, c, :], V[:, 1, c, :], c == 0, c == NT - 1)
                last.then_inc(ring_used, 1)

            def phase3(g, r, first_group, last_group):
                t, j = QT * g + r, r % 2
                final = last_group and r == QT - 1
                if not final:
                    if r == QT - 1:
                        pe.wait_ge(qt_lo, DT * g + 2 * DT)
                    for n in range(NQ - 1):
                        z_bank(t + 1, (r + 1) % QT, n)
                pe.wait_ge(prob_ready, t + 1)
                transpose_p(j, 0)
                if not final:
                    z_bank(t + 1, (r + 1) % QT, NQ - 1)
                if r == QT - 2 and not last_group:
                    pe.wait_ge(lo_ready, NQ * t + RING3 + 1)
                    q_group(g + 1)
                    pe.wait_ge(qt_lo, DT * g + 2 * DT)
                if not (first_group and r < 2):
                    pe.wait_ge(relu_ready, t - 1)
                for q in range(NQ):
                    if q < NQ - 1:
                        transpose_p(j, q + 1)
                    pv(t, j, q)

            q_group(0)
            pe.wait_ge(qt_lo, DT)
            for n in range(NQ):
                z_bank(0, 0, n)
            pe.wait_ge(v_ready, NT)
            for r in range(QT):
                phase3(0, r, True, False)
            with pe.Fori(1, QT - 1) as g:
                for r in range(QT):
                    phase3(g, r, False, False)
            for r in range(QT):
                phase3(QT - 1, r, False, True)

        @block.scalar
        def _(act):
            def s_hi(act, m, q):
                if not (isinstance(m, int) and m == 0 and q < 2):
                    act.wait_ge(ring_used, NQ * m + q - 1)
                nc.scalar.activation(ring_hi[q % 2][:, :, :], S[:, QT * q:QT * q + QT, ds(m * P, P)],
                                     ACT.Copy).then_inc(hi_ready, 1)

            def t_hi(act, m, ring0, q):
                act.wait_ge(blocks_T, NQ * m + ring0 - RING2 + q + 1)
                act.wait_ge(ring_used, NQ * m + ring0 + q - 1)
                nc.scalar.activation(ring_hi[q % 2][:, :, :], TB[q % 2][:, :].rearrange("p (k n) -> p k n", k=QT),
                                     ACT.Copy).then_inc(hi_ready, 1)

            n_done = 0
            for n, (r, b, c0_, c1_) in enumerate(STEPS0):
                if r == 8 and b == 0:
                    act.wait_ge(shift0_ready, 1)
                    for t in range(NT):
                        nc.scalar.activation(H0[:, t, :], H0[:, t, :], ACT.Relu, bias=shift0[:, t:t + 1],
                                             scale=rstd0[:, t:t + 1]).then_inc(h0_ready, 1)
                if r < ACT_SUMS:
                    for c in range(c0_, below(r, c1_)):
                        act.wait_ge(s_added, n + 1)
                        if n_done:
                            act.wait_ge(parts_act, n_done)
                        nc.scalar.activation(junk0[:, :], S[:, c, r * P:(r + 1) * P], ACT.Copy,
                                             accum_out=row_parts[:, c, NQ + r:NQ + r + 1]).then_inc(parts_act, 1)
                        n_done += 1
            act.wait_ge(dinv_ready, 1)
            act.wait_ge(h0_ready, NT)
            for t in range(NT):
                nc.scalar.activation(G_hi[:, t, :], H0[:, t, :], ACT.Copy, scale=dinv[:, t:t + 1]).then_inc(g_hi_ready, 1)
                if t == 0:
                    act.wait_ge(deg_step, 2)
                    s_hi(act, 0, 0)
                if t == 4:
                    s_hi(act, 0, 1)

            def u_hi(m, j):
                act.wait_ge(ring_used, NQ * m + NQ)
                nc.scalar.activation(U[:, 0:QT, ds(m * P, P)], Y[j][:, :].rearrange("p (c n) -> p c n", c=QT), ACT.Copy,
                                     scale=half_dinv[:, ds(m, 1)]).then_inc(u_hi_ready, 1)

            act.wait_ge(hdinv_ready, 1)
            s_hi(act, 0, 2)
            s_hi(act, 0, 3)

            def phase1(m, j):
                s_hi(act, m, 0)
                s_hi(act, m, 1)
                u_hi(m - 1, 1 - j)
                s_hi(act, m, 2)
                s_hi(act, m, 3)

            phase1(1, 1)
            with act.Fori(1, NT // 2) as i:
                for j in range(2):
                    phase1(2 * i + j, j)
            u_hi(NT - 1, 1)

            for a in range(DT):
                act.wait_ge(wprod_done, a + 1)
                nc.scalar.activation(M_w[:, 0, a, :], Z[a][:, :], ACT.Copy, scale=SCALE).then_inc(wprod_hi, 1)
            for a in range(DT):
                act.wait_ge(wprod_done, DT + a + 1)
                nc.scalar.activation(WvT[:, 0, a, :], Z[a][:, :], ACT.Copy).then_inc(wprod_hi, 1)

            def h_hi(m, j):
                act.wait_ge(h_T, m + 1)
                nc.scalar.activation(HT[:, 0:DT, ds(m * P, P)], Z[j][:, :].rearrange("p (a n) -> p a n", a=DT),
                                     ACT.Relu).then_inc(hT_hi, 1)

            def phase2(m, j):
                for q in range(1, NQ):
                    t_hi(act, m, RING2, q)
                if not isinstance(m, int) or m >= 1:
                    h_hi(m - 1, 1 - j)
                if not isinstance(m, int) or m < NT - 1:
                    t_hi(act, m + 1, RING2, 0)

            t_hi(act, 0, RING2, 0)
            for m in range(2):
                phase2(m, m)
            with act.Fori(1, NT // 2 - 1) as i:
                for j in range(2):
                    phase2(2 * i + j, j)
            for m in range(NT - 2, NT):
                phase2(m, m % 2)

            for t in range(NT):
                if t == 2:
                    h_hi(NT - 1, 1)
                act.wait_ge(vsum_ready, t + 1)
                nc.scalar.activation(V[:, 0, t, :], x_out[:, t % 2, :], ACT.Copy).then_inc(v_hi_ready, 1)

            def q_hi(g):
                for a in range(DT):
                    act.wait_ge(qt_done, DT * g + a + 1)
                    nc.scalar.activation(QT_[:, 0, a, :], TB[a % 2][:, :], ACT.Identity,
                                         bias=qbias[:, a:a + 1]).then_inc(qt_hi, 1)

            def exps(t, j):
                act.wait_ge(nmax_ready, t + 1)
                nc.scalar.activation(prob[j][:, :], prob[j][:, :], ACT.Exp, bias=nmax[:, j:j + 1],
                                     accum_out=rowsum[:, j:j + 1]).then_inc(prob_ready, 1)

            def relu(t, j):
                act.wait_ge(ring_used, NQ * t + RING3 + NQ)
                act.wait_ge(rinv_ready, t + 1)
                if not isinstance(t, int) or t >= 2:
                    act.wait_ge(out_stored[j], 8 * (t - j))
                nc.scalar.activation(x_out[:, j, :], Y[j][:, :], ACT.Relu,
                                     scale=rinv[:, j:j + 1]).then_inc(relu_ready, 1)

            def phase3(g, r, first_group, last_group):
                t, j = QT * g + r, r % 2
                if not (first_group and r == 0):
                    relu(t - 1, 1 - j)
                t_hi(act, t, RING3, 0)
                if r == QT - 2 and not last_group:
                    q_hi(g + 1)
                t_hi(act, t, RING3, 1)
                if not (last_group and r == QT - 1):
                    exps(t + 1, 1 - j)
                t_hi(act, t, RING3, 2)
                t_hi(act, t, RING3, 3)

            q_hi(0)
            exps(0, 0)
            for r in range(QT):
                phase3(0, r, True, False)
            with act.Fori(1, QT - 1) as g:
                for r in range(QT):
                    phase3(g, r, False, False)
            for r in range(QT):
                phase3(QT - 1, r, False, True)
            relu(NT - 1, 1)

        @block.vector
        def _(dve):
            def s_lo(dve, m, q):
                dve.wait_ge(hi_ready, NQ * m + q + 1)
                nc.vector.tensor_tensor(ring_lo[q % 2][:, :, :], S[:, QT * q:QT * q + QT, ds(m * P, P)],
                                        ring_hi[q % 2][:, :, :].bitcast(f32), ALU.subtract).then_inc(lo_ready, 1)

            def t_lo(dve, m, ring0, q):
                dve.wait_ge(hi_ready, NQ * m + ring0 + q + 1)
                nc.vector.tensor_tensor(ring_lo[q % 2][:, :, :], TB[q % 2][:, :].rearrange("p (k n) -> p k n", k=QT),
                                        ring_hi[q % 2][:, :, :].bitcast(f32), ALU.subtract).then_inc(lo_ready, 1)

            nc.vector.memset(neg_half[:, :], -0.5).then_inc(half_ready, 1)
            nc.vector.memset(row_parts[:, :, :], 0.0).then_inc(diag_ready, 1)
            dve.wait_ge(diag_ready, 1)

            def stats(t):
                nc.vector.bn_stats(bn0[:, t, :], H0[:, t, :]).then_inc(bn0_ready, 1)

            n_diag = 1
            for n, (r, b, c0_, c1_) in enumerate(STEPS0):
                if b == 0:
                    if r in (1, 2, 3, 4):
                        dve.wait_ge(x_all_in, 16 * 4) if r == 4 else None
                    if 4 <= r < 8:
                        for t in range(4 * (r - 4), 4 * (r - 4) + 4):
                            stats(t)
                dve.wait_ge(t0_done, n + 1)
                up, low = bank[2 * (n % 4)], bank[2 * (n % 4) + 1]
                cb = below(r, c1_)
                if cb > c0_:
                    dst = S[:, c0_:cb, r * P:(r + 1) * P]
                    nc.vector.tensor_tensor(dst, up[:, 0:(cb - c0_) * P].rearrange("p (c n) -> p c n", n=P), dst, ALU.add)
                if c1_ == r + 1:
                    if r == 0:
                        dve.wait_ge(ident_ready, 1)
                    dgl = S[:, r, r * P:(r + 1) * P]
                    nc.vector.scalar_tensor_tensor(dgl, ident[:, :], 2.0, dgl, ALU.mult, ALU.add).then_inc(diag_ready, 1)
                    n_diag += 1
                    dve.wait_ge(diag_ready, n_diag)
                dst = S[:, r, c0_ * P:c1_ * P]
                nc.vector.scalar_tensor_tensor(dst, low[:, 0:(c1_ - c0_) * P], 1.0, dst, ALU.mult, ALU.add,
                                               accum_out=row_parts[:, r, b:b + 1]).then_inc(s_added, 1)
                if r >= ACT_SUMS and cb > c0_:
                    dve.wait_ge(s_added, n + 1)
                    nc.vector.tensor_reduce(row_parts[:, c0_:cb, NQ + r], S[:, c0_:cb, r * P:(r + 1) * P],
                                            AX, ALU.add).then_inc(diag_ready, 1)
                    n_diag += 1
                if r == 8 - 1 and c1_ == r + 1:
                    dve.wait_ge(bn0_ready, NT)
                    for t in range(NT):
                        nc.vector.bn_aggr(mv0[:, t, :], bn0[:, t, :]).then_inc(mv0_ready, 1)
                    dve.wait_ge(mv0_ready, NT)
                    nc.vector.tensor_scalar(rstd0[:, :], mv0[:, :, 1], EPS, None, ALU.add).then_inc(var0_ready, 1)
                    dve.wait_ge(rstd0_ready, 1)
                    nc.vector.scalar_tensor_tensor(shift0[:, :], mv0[:, :, 0], -1.0, rstd0[:, :], ALU.mult, ALU.mult)\
                        .then_inc(shift0_ready, 1)

            dve.wait_ge(diag_ready, n_diag)
            dve.wait_ge(s_added, len(STEPS0))
            dve.wait_ge(parts_act, sum(r for r in range(ACT_SUMS)))
            nc.vector.tensor_reduce(deg[:, :], row_parts[:, :, :], AX, ALU.add).then_inc(deg_step, 1)
            dve.wait_ge(deg_step, 1)
            nc.vector.tensor_scalar(deg_pos[:, :], deg[:, :], 0.0, None, ALU.is_gt).then_inc(deg_step, 1)
            nc.vector.tensor_scalar(dinv[:, :], deg[:, :], 0.5, TINY, ALU.mult, ALU.max).then_inc(deg_step, 1)
            dve.wait_ge(dpow_ready, 1)
            nc.vector.tensor_tensor(dinv[:, :], deg[:, :], deg_pos[:, :], ALU.mult).then_inc(dinv_ready, 1)
            dve.wait_ge(dinv_ready, 1)
            nc.vector.tensor_scalar(half_dinv[:, :], dinv[:, :], 0.5, None, ALU.mult).then_inc(hdinv_ready, 1)

            for t in range(NT):
                dve.wait_ge(g_hi_ready, t + 1)
                nc.vector.scalar_tensor_tensor(G_lo[:, t, :], H0[:, t, :], dinv[:, t:t + 1], G_hi[:, t, :].bitcast(f32),
                                               ALU.mult, ALU.subtract).then_inc(g_ready, 1)
                if t == 0:
                    s_lo(dve, 0, 0)
                if t == 4:
                    s_lo(dve, 0, 1)

            def u_lo(m, j):
                dve.wait_ge(u_hi_ready, m + 1)
                nc.vector.scalar_tensor_tensor(U[:, QT:2 * QT, ds(m * P, P)], Y[j][:, :].rearrange("p (c n) -> p c n", c=QT),
                                               half_dinv[:, ds(m, 1)], U[:, 0:QT, ds(m * P, P)].bitcast(f32),
                                               ALU.mult, ALU.subtract).then_inc(u_ready, 1)

            def phase1(m, j):
                s_lo(dve, m, 0)
                s_lo(dve, m, 1)
                u_lo(m - 1, 1 - j)
                s_lo(dve, m, 2)
                s_lo(dve, m, 3)

            s_lo(dve, 0, 2)
            s_lo(dve, 0, 3)
            phase1(1, 1)
            with dve.Fori(1, NT // 2) as i:
                for j in range(2):
                    phase1(2 * i + j, j)
            dve.wait_ge(bias_in, 48)
            dve.wait_ge(w_in, 16 * 6)
            for e in range(DT):
                nc.vector.tensor_copy(bk_rep(e), bk_col[:, e:e + 1].to_broadcast([P, P])).then_inc(bk_rep_ready, 1)
            u_lo(NT - 1, 1)

            dve.wait_ge(wsmall_done, 1)
            nc.vector.tensor_scalar(qbias[:, :], TB[0][:, 0:DT], SCALE, None, ALU.mult)
            nc.vector.tensor_scalar(c0[:, :], TB[0][:, DT:DT + 1], SCALE, None, ALU.mult).then_inc(wsmall_ready, 1)
            nc.vector.tensor_scalar(wrow[:, :], TB[1][:, :], SCALE, None, ALU.mult).then_inc(wsmall_ready, 1)
            for a in range(DT):
                dve.wait_ge(wprod_hi, a + 1)
                nc.vector.scalar_tensor_tensor(M_w[:, 1, a, :], Z[a][:, :], SCALE, M_w[:, 0, a, :].bitcast(f32),
                                               ALU.mult, ALU.subtract).then_inc(wprod_lo, 1)
            for a in range(DT):
                dve.wait_ge(wprod_hi, DT + a + 1)
                nc.vector.tensor_tensor(WvT[:, 1, a, :], Z[a][:, :], WvT[:, 0, a, :].bitcast(f32),
                                        ALU.subtract).then_inc(wprod_lo, 1)
            dve.wait_ge(wsmall_ready, 2)

            def stats1(m, j):
                dve.wait_ge(ring_used, NQ * m + RING2 + NQ)
                if isinstance(m, int):
                    dve.wait_ge(xt_in[j], 16 * (m // 2 + 1))
                else:
                    dve.wait_ge(xt_in[j], 8 * (m - j) + 16)
                if not isinstance(m, int) or m >= 2:
                    dve.wait_ge(x1_stored[j], 8 * (m - j))
                nc.vector.tensor_tensor(x_out[:, j, :], Y[j][:, :], x_in[:, j, :], ALU.add)\
                    .then_inc(x1_ready, 1)
                dve.wait_ge(x1_ready, m + 1)
                nc.vector.bn_stats(bn[:, 6 * j:6 * j + 6], x_out[:, j, :]).then_inc(bn_ready, 1)
                dve.wait_ge(half_ready, 1)
                dve.wait_ge(bn_ready, m + 1)
                nc.vector.bn_aggr(mv[:, 2 * j:2 * j + 2], bn[:, 6 * j:6 * j + 6]).then_inc(mv_ready, 1)
                dve.wait_ge(mv_ready, m + 1)
                nc.vector.tensor_scalar(vareps[:, j:j + 1], mv[:, 2 * j + 1:2 * j + 2], EPS, None, ALU.add)\
                    .then_inc(var_ready, 1)

            def norm1(m, j):
                dve.wait_ge(rstd_ready, m + 1)
                if not isinstance(m, int) or m >= 2:
                    dve.wait_ge(h_T, m - 1)
                nc.vector.tensor_scalar(normed[:, j, :], x_out[:, j, :], mv[:, 2 * j:2 * j + 1], rstd[:, j:j + 1],
                                        ALU.subtract, ALU.mult).then_inc(norm_ready, 1)
                dve.wait_ge(norm_ready, m + 1)
                if not isinstance(m, int) or m >= 1:
                    dve.wait_ge(cdot_ready, m)
                nc.vector.scalar_tensor_tensor(junk[:, :], normed[:, j, :], 0.0, wrow[:, :], ALU.max, ALU.mult,
                                               accum_out=cbias[:, ds(m, 1)]).then_inc(cdot_ready, 1)

            def h_lo(m, j):
                dve.wait_ge(hT_hi, m + 1)
                nc.vector.scalar_tensor_tensor(HT[:, DT:2 * DT, ds(m * P, P)], Z[j][:, :].rearrange("p (a n) -> p a n", a=DT),
                                               0.0, HT[:, 0:DT, ds(m * P, P)].bitcast(f32),
                                               ALU.max, ALU.subtract).then_inc(hT_lo, 1)

            def phase2(m, j):
                later = not isinstance(m, int) or m >= 1
                t_lo(dve, m, RING2, 1)
                if later:
                    stats1(m - 1, 1 - j)
                t_lo(dve, m, RING2, 2)
                if later:
                    norm1(m - 1, 1 - j)
                t_lo(dve, m, RING2, 3)
                if later:
                    h_lo(m - 1, 1 - j)
                if not isinstance(m, int) or m < NT - 1:
                    t_lo(dve, m + 1, RING2, 0)

            t_lo(dve, 0, RING2, 0)
            for m in range(2):
                phase2(m, m)
            with dve.Fori(1, NT // 2 - 1) as i:
                for j in range(2):
                    phase2(2 * i + j, j)
            for m in range(NT - 2, NT):
                phase2(m, m % 2)
            stats1(NT - 1, 1)
            norm1(NT - 1, 1)
            dve.wait_ge(cdot_ready, NT)
            nc.vector.tensor_scalar(cbias[:, :], cbias[:, :], c0[:, 0:1], None, ALU.add).then_inc(cbias_ready, 1)

            for j in range(2):
                dve.wait_ge(x1_stored[j], 16 * NT // 2)
            for t in range(NT):
                if t == 2:
                    h_lo(NT - 1, 1)
                dve.wait_ge(v_done, t + 1)
                if t >= 2:
                    dve.wait_ge(v_ready, t - 1)
                nc.vector.tensor_tensor(x_out[:, t % 2, :], Y[t % 2][:, :], bv_row[:, :], ALU.add)\
                    .then_inc(vsum_ready, 1)
                dve.wait_ge(vsum_ready, t + 1)
                dve.wait_ge(v_hi_ready, t + 1)
                nc.vector.tensor_tensor(V[:, 1, t, :], x_out[:, t % 2, :], V[:, 0, t, :].bitcast(f32),
                                        ALU.subtract).then_inc(v_ready, 1)

            def q_lo(g):
                for a in range(DT):
                    dve.wait_ge(qt_hi, DT * g + a + 1)
                    nc.vector.scalar_tensor_tensor(QT_[:, 1, a, :], TB[a % 2][:, :], qbias[:, a:a + 1],
                                                   QT_[:, 0, a, :].bitcast(f32), ALU.add, ALU.subtract).then_inc(qt_lo, 1)

            def score(t, j, n):
                dve.wait_ge(z_done, NQ * t + n + 1)
                if n == 0:
                    dve.wait_ge(adj_in, 16 * t + 16)
                    if not isinstance(t, int) or t >= 2:
                        dve.wait_ge(blocks_T, NQ * t + RING3 - RING2 - NQ)
                s = prob[j][:, n * D:(n + 1) * D]
                nc.vector.scalar_tensor_tensor(s, Z[n][:, :], cbias[:, ds(t, 1)], adj_row[:, n * D:(n + 1) * D],
                                               ALU.add, ALU.mult).then_inc(s_ready, 1)
                dve.wait_ge(s_ready, NQ * t + n + 1)
                if not (isinstance(t, int) and t == 0 and n == 0):
                    dve.wait_ge(masked_ready, NQ * t + n)
                nc.vector.tensor_scalar(junk[:, :], s, 0.0, MASKED, ALU.is_equal, ALU.mult).then_inc(mask_ready, 1)
                dve.wait_ge(mask_ready, NQ * t + n + 1)
                nc.vector.tensor_tensor(s, s, junk[:, :], ALU.add).then_inc(masked_ready, 1)

            def row_max(t, j):
                dve.wait_ge(masked_ready, NQ * t + NQ)
                nc.vector.tensor_reduce(nmax[:, j:j + 1], prob[j][:, :], AX, ALU.max, negate=True)\
                    .then_inc(nmax_ready, 1)

            def finish(t, j):
                dve.wait_ge(relu_ready, t + 1)
                if isinstance(t, int):
                    dve.wait_ge(x1_in[j], 16 * (t // 2 + 1))
                else:
                    dve.wait_ge(x1_in[j], 8 * (t - j) + 16)
                nc.vector.tensor_tensor(x_out[:, j, :], x_out[:, j, :], x_in[:, j, :], ALU.add).then_inc(out_ready, 1)

            def phase3(g, r, first_group, last_group):
                t, j = QT * g + r, r % 2
                final = last_group and r == QT - 1
                dve.wait_ge(prob_ready, t + 1)
                nc.vector.reciprocal(rinv[:, j:j + 1], rowsum[:, j:j + 1]).then_inc(rinv_ready, 1)
                if not (first_group and r == 0):
                    finish(t - 1, 1 - j)
                if not final:
                    for n in range(NQ - 1):
                        score(t + 1, 1 - j, n)
                t_lo(dve, t, RING3, 0)
                if not final:
                    score(t + 1, 1 - j, NQ - 1)
                if r == QT - 2 and not last_group:
                    q_lo(g + 1)
                t_lo(dve, t, RING3, 1)
                if not final:
                    row_max(t + 1, 1 - j)
                t_lo(dve, t, RING3, 2)
                t_lo(dve, t, RING3, 3)

            q_lo(0)
            dve.wait_ge(cbias_ready, 1)
            for n in range(NQ):
                score(0, 0, n)
            row_max(0, 0)
            for r in range(QT):
                phase3(0, r, True, False)
            with dve.Fori(1, QT - 1) as g:
                for r in range(QT):
                    phase3(g, r, False, False)
            for r in range(QT):
                phase3(QT - 1, r, False, True)
            finish(NT - 1, 1)

        @block.gpsimd
        def _(pool):
            nc.gpsimd.memset(ident[:, :], 0.0).then_inc(ident_step, 1)
            pool.wait_ge(ident_step, 1)
            nc.gpsimd.affine_select(out=ident[:, :], in_=ident[:, :], compare_op=ALU.not_equal, fill=1.0, base=0,
                                    pattern=[[-1, P]], channel_multiplier=1).then_inc(ident_ready, 1)
            pool.wait_ge(half_ready, 1)
            pool.wait_ge(var0_ready, 1)
            nc.gpsimd.tensor_tensor(rstd0[:, :], rstd0[:, :], neg_half[:, :], ALU.pow).then_inc(rstd0_ready, 1)
            pool.wait_ge(deg_step, 3)
            nc.gpsimd.tensor_tensor(deg[:, :], dinv[:, :], neg_half[:, :], ALU.pow).then_inc(dpow_ready, 1)

            def rstds(m, j):
                pool.wait_ge(var_ready, m + 1)
                nc.gpsimd.tensor_tensor(rstd[:, j:j + 1], vareps[:, j:j + 1], neg_half[:, 0:1], ALU.pow)\
                    .then_inc(rstd_ready, 1)

            with pool.Fori(0, NT // 2) as i:
                for j in range(2):
                    rstds(2 * i + j, j)


_INS = ["x", "adj", "L1_gnn_W_q", "L1_gnn_b_q", "L1_gnn_W_k", "L1_gnn_b_k", "L1_gnn_W_v", "L1_gnn_b_v"]


def kernel(**inputs):
    import numpy as _np
    import concourse.bacc as _bacc
    from concourse import mybir as _mybir
    from concourse.bass_utils import run_bass_kernel_spmd as _run

    nc = _bacc.Bacc("TRN2", target_bir_lowering=False, num_devices=1)
    arrays, args = {}, []
    for name in _INS:
        a = _np.ascontiguousarray(inputs[name])
        arrays[f"in_{name}"] = a
        args.append(nc.dram_tensor(f"in_{name}", a.shape, _mybir.dt.from_np(a.dtype), kind="ExternalInput").ap())
    out = nc.dram_tensor("x2", (N, D), _mybir.dt.float32, kind="ExternalOutput").ap()
    build(nc, *args, out)
    r = _run(nc, [arrays], core_ids=[0])
    return r.results[0]["x2"]
```

```python
import concourse.bass as bass
from concourse import mybir
from concourse.alu_op_type import AluOpType as ALU
from contextlib import ExitStack

N = 2048
D = 512
P = 128
NT = N // P
DT = D // P
QT = 4
NQ = NT // QT
EPS = 1e-5
MASKED = -10000.0
SCALE = 1.0 / float(D) ** 0.5
TINY = 1.17549435e-38


def build(nc, x, adj, w_q, b_q, w_k, b_k, w_v, b_v, out):
    f32, f32r = mybir.dt.float32, mybir.dt.float32r
    ACT = mybir.ActivationFunctionType
    AX = mybir.AxisListType.X
    ds = bass.ds

    x_t = x.rearrange("(t p) d -> p t d", p=P)
    wq_t = w_q.rearrange("(t p) d -> p t d", p=P)
    wk_t = w_k.rearrange("(t p) d -> p t d", p=P)
    wv_t = w_v.rearrange("(t p) d -> p t d", p=P)
    x1_dram = nc.dram_tensor("x1_scratch", [N, D], f32).ap()

    BASE = (nc.sbuf_base + 31) // 32 * 32
    KB = 1024
    REG_S = BASE
    REG_G = REG_S + 128 * KB
    REG_R = REG_G + 64 * KB

    def at(name, shape, dt, offset):
        return nc.alloc_sbuf_tensor_at(name, shape, dt, offset=offset)

    S = at("S", [P, NT, N], f32, REG_S)
    U = at("U", [P, NT // 2, N], f32r, REG_S)
    W = at("W", [P, NT // 2, N], f32, REG_S + 64 * KB)
    HT = at("HT", [P, 2 * DT, N], f32r, REG_S + 64 * KB)
    V = at("V", [P, 2, NT, D], f32r, REG_S)
    H0 = at("H0", [P, NT, D], f32, REG_G + 32 * KB)
    G_hi = at("G_hi", [P, NT, D], f32r, REG_G)
    G_lo = at("G_lo", [P, NT, D], f32r, REG_G + 32 * KB)
    A_row = at("A_row", [P, 2, N], f32, REG_G)
    M_w = at("M_w", [P, 2, DT, D], f32r, REG_G + 16 * KB)
    WvT = at("WvT", [P, 2, DT, D], f32r, REG_G + 32 * KB)
    x_in = at("x_in", [P, 2, D], f32, REG_G + 48 * KB)
    x_out = at("x_out", [P, 2, D], f32, REG_G + 52 * KB)
    normed = at("normed", [P, 2, D], f32, REG_G + 56 * KB)
    adj_row = at("adj_row", [P, N], f32, REG_G + 32 * KB)
    prob = [at("prob0", [P, N], f32, REG_G + 40 * KB), at("prob1", [P, N], f32, REG_G + 56 * KB)]
    q_T = at("q_T", [P, 2, DT, D], f32r, REG_G)
    ring_hi = [at(f"ring_hi{b}", [P, QT, P], f32r, REG_R + 2 * KB * b) for b in range(2)]
    ring_lo = [at(f"ring_lo{b}", [P, QT, P], f32r, REG_R + 4 * KB + 2 * KB * b) for b in range(2)]
    PARTS = NQ + NT
    row_parts = at("row_parts", [P, NT, PARTS], f32, REG_G + 30 * KB)
    bn0 = at("bn0", [P, NT, 6], f32, REG_G + 29 * KB)
    mv0 = at("mv0", [P, NT, 2], f32, REG_G + 28 * KB)
    ident2 = at("ident2", [P, P], f32, REG_G + 27 * KB)
    ident = at("ident", [P, P], f32, REG_R + 8 * KB)
    wrow = at("wrow", [P, D], f32, REG_R + 8 * KB + 512)
    bv_row = at("bv_row", [P, D], f32, REG_R + 10 * KB + 512)
    junk = at("junk", [P, D], f32, REG_R + 12 * KB + 512)
    small = REG_R + 14 * KB + 512
    cols = {}
    for name, n in (("neg_half", NT), ("deg", NT), ("deg_pos", NT), ("dinv", NT), ("half_dinv", NT),
                    ("rstd0", NT), ("shift0", NT), ("cbias", NT), ("bq_col", DT), ("bk_col", DT),
                    ("qbias", DT), ("c0", 1), ("bqk", 1), ("bqk4", DT), ("bn", 12), ("mv", 4), ("vareps", 2), ("rstd", 2),
                    ("mx4", 8), ("q_junk", 1), ("nmax", 2), ("rowsum", 2), ("rinv", 2)):
        cols[name] = at(name, [P, n], f32, small)
        small += (4 * n + 31) // 32 * 32
    assert small <= nc.sbuf_usable_end, (small, nc.sbuf_usable_end)
    neg_half, deg, deg_pos, dinv, half_dinv = (cols[k] for k in ("neg_half", "deg", "deg_pos", "dinv", "half_dinv"))
    rstd0, shift0, cbias, bq_col, bk_col = (cols[k] for k in ("rstd0", "shift0", "cbias", "bq_col", "bk_col"))
    qbias, c0, bn, mv, vareps, rstd = (cols[k] for k in ("qbias", "c0", "bn", "mv", "vareps", "rstd"))
    bqk, bqk4 = cols["bqk"], cols["bqk4"]
    mx4, nmax, rowsum, rinv = (cols[k] for k in ("mx4", "nmax", "rowsum", "rinv"))

    W_r = at("W_r", [P, NT // 2, N], f32r, REG_S + 64 * KB)

    def w_place(tensor, n, t):
        return tensor[:, 2 * n + t // 2, (t % 2) * D:(t % 2 + 1) * D]

    def w_tile(n, t):
        return w_place(W, n, t)

    def w_lo(n, t):
        return w_place(W_r, n, t)

    def w_hi(n, t):
        return W_r[:, DT * n + t, 2 * D:3 * D]

    def bias_sum(n):
        return W[:, 6, n * D:(n + 1) * D]

    def bias_lo(n):
        return W_r[:, 6, n * D:(n + 1) * D]

    def bias_hi(n):
        return W_r[:, 7, n * D:(n + 1) * D]

    ones_r = W_r[:, 0, 3 * D:3 * D + P]
    ones = W[:, 1, 3 * D:3 * D + P]

    ctx = ExitStack()
    with ctx:
        bank = [ctx.enter_context(nc.psum_tensor(f"bank{i}", [P, D], f32)) for i in range(8)]
        Z, TB, Y = bank[0:4], bank[4:6], bank[6:8]

        def sem(name):
            return ctx.enter_context(nc.semaphore(name))

        a_in = [sem(f"a_in{r}") for r in range(NT)]
        x_in0 = [sem(f"x_in0_{k}") for k in range(4)]
        bias_in = sem("bias_in")
        w_in = sem("w_in")
        arow_in = [sem(f"arow_in{i}") for i in range(2)]
        xt_in = [sem(f"xt_in{i}") for i in range(2)]
        x1_stored = [sem(f"x1_stored{i}") for i in range(2)]
        adj_in = sem("adj_in")
        x1_in = [sem(f"x1_in{i}") for i in range(2)]
        out_stored = [sem(f"out_stored{i}") for i in range(2)]
        ident_step, ident_ready, half_ready = sem("ident_step"), sem("ident_ready"), sem("half_ready")
        t0_done, s_added, parts_act, mirror_done = (sem(k) for k in ("t0_done", "s_added", "parts_act", "mirror_done"))
        parts_zero, parts_dve, ident2_ready = sem("parts_zero"), sem("parts_dve"), sem("ident2_ready")
        bn0_ready, mv0_ready, var0_ready, rstd0_ready, shift0_ready = (
            sem(k) for k in ("bn0_ready", "mv0_ready", "var0_ready", "rstd0_ready", "shift0_ready"))
        h0_ready, deg_step, dpow_ready, dinv_ready, hdinv_ready = (
            sem(k) for k in ("h0_ready", "deg_step", "dpow_ready", "dinv_ready", "hdinv_ready"))
        g_hi_ready, g_ready = sem("g_hi_ready"), sem("g_ready")
        hi_ready, lo_ready, ring_used = sem("hi_ready"), sem("lo_ready"), sem("ring_used")
        blocks_T = sem("blocks_T")
        u_hi_ready, u_ready = sem("u_hi_ready"), sem("u_ready")
        w_hi_ready, w_lo_ready, ones_ready = sem("w_hi_ready"), sem("w_lo_ready"), sem("ones_ready")
        bsum_step, bsum_hi_ready, bsum_lo_ready, bqk_ready = (
            sem(k) for k in ("bsum_step", "bsum_hi_ready", "bsum_lo_ready", "bqk_ready"))
        wsmall_done, wsmall_ready = sem("wsmall_done"), sem("wsmall_ready")
        wprod_done, wprod_hi, wprod_lo = sem("wprod_done"), sem("wprod_hi"), sem("wprod_lo")
        x1_ready, bn_ready, mv_ready, var_ready, rstd_ready, norm_ready = (
            sem(k) for k in ("x1_ready", "bn_ready", "mv_ready", "var_ready", "rstd_ready", "norm_ready"))
        cdot_ready, cbias_ready = sem("cdot_ready"), sem("cbias_ready")
        h_T, hT_hi, hT_lo = sem("h_T"), sem("hT_hi"), sem("hT_lo")
        v_done = sem("v_done")
        vsum_ready, v_hi_ready, v_ready = sem("vsum_ready"), sem("v_hi_ready"), sem("v_ready")
        qt_done, qt_hi, qt_lo = sem("qt_done"), sem("qt_hi"), sem("qt_lo")
        z_done, s_ready, mask_ready, masked_ready = sem("z_done"), sem("s_ready"), sem("mask_ready"), sem("masked_ready")
        rmax_ready, nmax_ready, prob_ready = sem("rmax_ready"), sem("nmax_ready"), sem("prob_ready")
        rinv_ready, relu_ready, out_ready = sem("rinv_ready"), sem("relu_ready"), sem("out_ready")

        RING2, RING3 = NT * NQ, 2 * NT * NQ

        def batches(r):
            return [(c, min(c + QT, r + 1)) for c in range(0, r + 1, QT)]

        STEPS0 = [(r, b, c0_, c1_) for r in range(NT) for b, (c0_, c1_) in enumerate(batches(r))]

        def below(r, c1_):
            return min(c1_, r)

        def by_dve(n):
            return STEPS0[n][0] >= DVE_SHARE and STEPS0[n][1] % 2 == 1

        def mirrors(n):
            return sum(below(r, c1_) - c0_ for k, (r, b, c0_, c1_) in enumerate(STEPS0[:n + 1]) if by_dve(k) == by_dve(n))

        def mirror_steps(n):
            return sum(below(r, c1_) > c0_ for r, b, c0_, c1_ in STEPS0[:n + 1])

        DVE_SHARE = 11

        def three(pe_out, hi_l, lo_l, hi_r, lo_r, first, last):
            nc.tensor.matmul(pe_out, hi_l, hi_r, start=first, stop=False)
            nc.tensor.matmul(pe_out, hi_l, lo_r, start=False, stop=False)
            return nc.tensor.matmul(pe_out, lo_l, hi_r, start=False, stop=last)

        block = ctx.enter_context(nc.Block())

        @block.sync
        def _(sp):
            for r in range(NT):
                sp.dma_start(S[:, r, :], adj[r * P:(r + 1) * P, :]).then_inc(a_in[r], 16)
                if r < 4:
                    sp.dma_start(H0[:, 4 * r:4 * r + 4, :], x_t[:, 4 * r:4 * r + 4, :]).then_inc(x_in0[r], 16)
            with nc.allow_non_contiguous_dma(reason="512 bias values, one a partition and tile"):
                sp.dma_start(bq_col[:, :], b_q.rearrange("(t p) -> p t", p=P)).then_inc(bias_in, 16)
                sp.dma_start(bk_col[:, :], b_k.rearrange("(t p) -> p t", p=P)).then_inc(bias_in, 16)
            sp.dma_start(bv_row[:, :], b_v.partition_broadcast(P)).then_inc(bias_in, 16)
            sp.wait_ge(lo_ready, NT // 2 * NQ)
            for n, w_dram in enumerate((wq_t, wk_t, wv_t)):
                for h in range(2):
                    sp.dma_start(W[:, 2 * n + h, 0:2 * D].rearrange("p (t d) -> p t d", t=2),
                                 w_dram[:, 2 * h:2 * h + 2, :]).then_inc(w_in, 16)
            sp.wait_ge(ring_used, RING2)

            def rows_in(m, j):
                sp.dma_start(A_row[:, j, :], adj[ds(m * P, P), :]).then_inc(arow_in[j], 16)
                sp.dma_start(x_in[:, j, :], x[ds(m * P, P), :]).then_inc(xt_in[j], 16)

            def x1_store(m, j):
                sp.wait_ge(x1_ready, m + 1)
                sp.dma_start(x1_dram[ds(m * P, P), :], x_out[:, j, :]).then_inc(x1_stored[j], 16)

            for m in range(2):
                rows_in(m, m)
            with sp.Fori(0, NT // 2 - 1) as i:
                for j in range(2):
                    m = 2 * i + j
                    sp.wait_ge(x1_ready, m + 1)
                    sp.wait_ge(blocks_T, NQ * m + NQ)
                    rows_in(m + 2, j)
                    x1_store(m, j)
            for m in range(NT - 2, NT):
                x1_store(m, m % 2)
            for j in range(2):
                sp.wait_ge(x1_stored[j], 16 * NT // 2)

            def adj_load(i):
                sp.dma_start(adj_row[:, :], adj[ds(i * P, P), :]).then_inc(adj_in, 16)

            def x1_load(i, j):
                sp.dma_start(x_in[:, j, :], x1_dram[ds(i * P, P), :]).then_inc(x1_in[j], 16)

            def out_store(i, j):
                sp.wait_ge(out_ready, i + 1)
                sp.dma_start(out[ds(i * P, P), :], x_out[:, j, :]).then_inc(out_stored[j], 16)

            x1_load(0, 0)
            x1_load(1, 1)
            sp.wait_ge(v_done, NT)
            adj_load(0)
            sp.wait_ge(s_ready, NQ)
            adj_load(1)
            with sp.Fori(0, NT // 2 - 1) as i:
                for j in range(2):
                    t = 2 * i + j
                    sp.wait_ge(s_ready, NQ * t + 2 * NQ)
                    adj_load(t + 2)
                    out_store(t, j)
                    x1_load(t + 2, j)
            for t in range(NT - 2, NT):
                out_store(t, t % 2)
            for j in range(2):
                sp.wait_ge(out_stored[j], 16 * NT // 2)

        @block.tensor
        def _(pe):
            pe.wait_ge(ident_ready, 1)
            def mirror(n):
                r, b, c0_, c1_ = STEPS0[n]
                if below(r, c1_) == c0_:
                    return
                pe.wait_ge(s_added, n + 1)
                if n >= 4 and mirrors(n - 4):
                    pe.wait_ge(parts_dve if by_dve(n - 4) else parts_act, mirrors(n - 4))
                for c in range(c0_, below(r, c1_)):
                    last = nc.tensor.transpose(bank[2 * (n % 4)][:, (c - c0_) * P:(c - c0_ + 1) * P],
                                               S[:, r, c * P:(c + 1) * P], ident[:, :])
                last.then_inc(mirror_done, 1)

            for n, (r, b, c0_, c1_) in enumerate(STEPS0):
                if b == 0:
                    pe.wait_ge(a_in[r], 16)
                if n >= 4:
                    pe.wait_ge(s_added, n - 3)
                low = bank[2 * (n % 4) + 1]
                for c in range(c0_, below(r, c1_)):
                    last = nc.tensor.transpose(low[:, (c - c0_) * P:(c - c0_ + 1) * P],
                                               S[:, c, r * P:(r + 1) * P], ident[:, :])
                if c1_ == r + 1:
                    if r == 0:
                        pe.wait_ge(ident2_ready, 1)
                    diag = low[:, (r - c0_) * P:(r - c0_ + 1) * P]
                    nc.tensor.matmul(diag, S[:, r, r * P:(r + 1) * P], ident[:, :], start=True, stop=False)
                    last = nc.tensor.matmul(diag, ident2[:, :], ident[:, :], start=False, stop=True)
                last.then_inc(t0_done, 1)
                if n:
                    mirror(n - 1)
            mirror(len(STEPS0) - 1)
            pe.wait_ge(s_added, len(STEPS0))

            def phase1(m, j):
                if not isinstance(m, int) or m >= 2:
                    pe.wait_ge(u_ready, m - 1)
                for q in range(NQ):
                    pe.wait_ge(lo_ready, NQ * m + q + 1)
                    for k in range(QT):
                        t = QT * q + k
                        if isinstance(m, int) and m == 0:
                            pe.wait_ge(g_ready, t + 1)
                        last = three(Y[j][:, :], ring_hi[q % 2][:, k, :], ring_lo[q % 2][:, k, :],
                                     G_hi[:, t, :], G_lo[:, t, :], t == 0, t == NT - 1)
                    last.then_inc(ring_used, 1)

            for m in range(2):
                phase1(m, m)
            with pe.Fori(1, NT // 2) as i:
                for j in range(2):
                    phase1(2 * i + j, j)

            pe.wait_ge(w_lo_ready, 2 * DT)
            for a in range(DT):
                rows = slice(a * P, (a + 1) * P)
                for e in range(DT):
                    last = three(Z[a][:, :], w_hi(0, e)[:, rows], w_lo(0, e)[:, rows], w_hi(1, e), w_lo(1, e),
                                 e == 0, e == DT - 1)
                last.then_inc(wprod_done, 1)
            pe.wait_ge(bsum_lo_ready, 2)
            pe.wait_ge(ones_ready, 2)
            for n in range(2):
                nc.tensor.matmul(TB[n][:, :], ones_r, bias_hi(n), start=True, stop=False)
                nc.tensor.matmul(TB[n][:, :], ones_r, bias_lo(n), start=False, stop=True)
            pe.wait_ge(u_ready, NT - 1)
            pe.wait_ge(bqk_ready, 1)
            nc.tensor.matmul(Y[0][:, 0:1], ones, bqk[:, :], start=True, stop=True).then_inc(wsmall_done, 1)
            for a in range(DT):
                pe.wait_ge(wprod_lo, a + 1)
                for e in range(DT):
                    last = nc.tensor.transpose(Z[a][:, e * P:(e + 1) * P], w_tile(2, e)[:, a * P:(a + 1) * P], ident[:, :])
                last.then_inc(wprod_done, 1)

            def transposes(q, j):
                for k in range(QT):
                    last = nc.tensor.transpose(TB[q % 2][:, k * P:(k + 1) * P],
                                               A_row[:, j, (QT * q + k) * P:(QT * q + k + 1) * P], ident[:, :])
                last.then_inc(blocks_T, 1)

            def transpose_h(m, j):
                pe.wait_ge(norm_ready, m + 1)
                if not isinstance(m, int) or m >= 2:
                    pe.wait_ge(hT_lo, m - 1)
                else:
                    pe.wait_ge(wprod_lo, 2 * DT)
                for a in range(DT):
                    last = nc.tensor.transpose(Z[j][:, a * P:(a + 1) * P], normed[:, j, a * P:(a + 1) * P], ident[:, :])
                last.then_inc(h_T, 1)

            def phase2(m, j):
                if not isinstance(m, int) or m >= 2:
                    pe.wait_ge(x1_ready, m - 1)
                for q in range(NQ):
                    if q < NQ - 1:
                        transposes(q + 1, j)
                    elif not isinstance(m, int) or m < NT - 1:
                        pe.wait_ge(arow_in[1 - j], arrived(m, j))
                        transposes(0, 1 - j)
                    if q == 2 and (not isinstance(m, int) or m >= 1):
                        transpose_h(m - 1, 1 - j)
                    pe.wait_ge(lo_ready, NQ * m + RING2 + q + 1)
                    for k in range(QT):
                        t = QT * q + k
                        u = U[:, :, t * P:(t + 1) * P]
                        last = three(Y[j][:, :].rearrange("p (c n) -> p c n", c=QT), ring_hi[q % 2][:, k, :], ring_lo[q % 2][:, k, :],
                                     u[:, 0:QT, :], u[:, QT:2 * QT, :], t == 0, t == NT - 1)
                    last.then_inc(ring_used, 1)

            def arrived(m, j):
                return 16 * ((m + 1) // 2 + 1) if isinstance(m, int) else 8 * (m - j) + 16 * j + 16

            pe.wait_ge(wsmall_ready, DT + 2)
            pe.wait_ge(arow_in[0], 16)
            transposes(0, 0)
            pe.wait_ge(u_ready, NT)
            for m in range(2):
                phase2(m, m)
            with pe.Fori(1, NT // 2 - 1) as i:
                for j in range(2):
                    phase2(2 * i + j, j)
            for m in range(NT - 2, NT):
                phase2(m, m % 2)

            def v_tile(t):
                pe.wait_ge(hT_lo, t + 1)
                if t < 2:
                    pe.wait_ge(x1_ready, NT - 1 + t)
                else:
                    pe.wait_ge(vsum_ready, t - 1)
                for a in range(DT):
                    rows = slice(t * P, (t + 1) * P)
                    last = three(Y[t % 2][:, :], HT[:, a, rows], HT[:, DT + a, rows],
                                 WvT[:, 0, a, :], WvT[:, 1, a, :], a == 0, a == DT - 1)
                last.then_inc(v_done, 1)

            def q_group(g):
                for a in range(DT):
                    if a >= 2:
                        pe.wait_ge(qt_lo, DT * g + a - 1)
                    for d in range(DT):
                        cols_g = ds(g * D, D)
                        last = three(TB[a % 2][:, :], M_w[:, 0, d, a * P:(a + 1) * P], M_w[:, 1, d, a * P:(a + 1) * P],
                                     HT[:, d, cols_g], HT[:, DT + d, cols_g], d == 0, d == DT - 1)
                    last.then_inc(qt_done, 1)

            def z_bank(t, r, n):
                pe.wait_ge(s_ready, NQ * t + n - (NQ - 1)) if not isinstance(t, int) or t >= 1 else None
                for d in range(DT):
                    last = three(Z[n][:, :], q_T[:, 0, d, r * P:(r + 1) * P], q_T[:, 1, d, r * P:(r + 1) * P],
                                 HT[:, d, n * D:(n + 1) * D], HT[:, DT + d, n * D:(n + 1) * D], d == 0, d == DT - 1)
                last.then_inc(z_done, 1)

            def transpose_p(j, q):
                for k in range(QT):
                    last = nc.tensor.transpose(TB[q % 2][:, k * P:(k + 1) * P],
                                               prob[j][:, (QT * q + k) * P:(QT * q + k + 1) * P], ident[:, :])
                last.then_inc(blocks_T, 1)

            def pv(t, j, q):
                for k in range(QT):
                    c = QT * q + k
                    last = three(Y[j][:, :], ring_hi[q % 2][:, k, :], ring_lo[q % 2][:, k, :],
                                 V[:, 0, c, :], V[:, 1, c, :], c == 0, c == NT - 1)
                last.then_inc(ring_used, 1)

            def phase3(g, r, first_group, last_group):
                t, j = QT * g + r, r % 2
                final = last_group and r == QT - 1
                if not final:
                    if r == QT - 1:
                        pe.wait_ge(qt_lo, DT * g + 2 * DT)
                    for n in range(NQ - 1):
                        z_bank(t + 1, (r + 1) % QT, n)
                pe.wait_ge(prob_ready, t + 1)
                if not (first_group and r == 0):
                    pe.wait_ge(lo_ready, NQ * t + RING3)
                transpose_p(j, 0)
                transpose_p(j, 1)
                if not final:
                    z_bank(t + 1, (r + 1) % QT, NQ - 1)
                q_next = r == QT - 2 and not last_group
                if q_next:
                    pe.wait_ge(lo_ready, NQ * t + RING3 + 2)
                    q_group(g + 1)
                if not (first_group and r < 2):
                    pe.wait_ge(relu_ready, t - 1)
                for q in range(NQ):
                    pe.wait_ge(lo_ready, NQ * t + RING3 + q + 1)
                    if q < NQ - 2:
                        if q_next:
                            pe.wait_ge(qt_lo, DT * g + 2 * DT - 1 + q)
                        transpose_p(j, q + 2)
                    pv(t, j, q)

            for t in range(NT):
                if t == 2:
                    transpose_h(NT - 1, 1)
                if t == NT - 2:
                    q_group(0)
                v_tile(t)
            pe.wait_ge(qt_lo, DT)
            for n in range(NQ):
                z_bank(0, 0, n)
            pe.wait_ge(v_ready, NT)
            for r in range(QT):
                phase3(0, r, True, False)
            with pe.Fori(1, QT - 1) as g:
                for r in range(QT):
                    phase3(g, r, False, False)
            for r in range(QT):
                phase3(QT - 1, r, False, True)

        @block.scalar
        def _(act):
            def s_hi(m, q):
                if not (isinstance(m, int) and m == 0 and q < 2):
                    act.wait_ge(ring_used, NQ * m + q - 1)
                nc.scalar.activation(ring_hi[q % 2][:, :, :], S[:, QT * q:QT * q + QT, ds(m * P, P)],
                                     ACT.Copy).then_inc(hi_ready, 1)

            def t_hi(m, ring0, q):
                act.wait_ge(blocks_T, NQ * m + ring0 - RING2 + q + 1)
                act.wait_ge(ring_used, NQ * m + ring0 + q - 1)
                nc.scalar.activation(ring_hi[q % 2][:, :, :], TB[q % 2][:, :].rearrange("p (k n) -> p k n", k=QT),
                                     ACT.Copy).then_inc(hi_ready, 1)

            act.wait_ge(parts_zero, 1)
            for n, (r, b, c0_, c1_) in enumerate(STEPS0):
                if r == 7 and b == 0:
                    act.wait_ge(shift0_ready, 1)
                    for t in range(NT):
                        nc.scalar.activation(H0[:, t, :], H0[:, t, :], ACT.Relu, bias=shift0[:, t:t + 1],
                                             scale=rstd0[:, t:t + 1]).then_inc(h0_ready, 1)
                if not by_dve(n) and below(r, c1_) > c0_:
                    act.wait_ge(mirror_done, mirror_steps(n))
                    for c in range(c0_, below(r, c1_)):
                        nc.scalar.activation(S[:, c, r * P:(r + 1) * P],
                                             bank[2 * (n % 4)][:, (c - c0_) * P:(c - c0_ + 1) * P], ACT.Copy,
                                             accum_out=row_parts[:, c, NQ + r:NQ + r + 1]).then_inc(parts_act, 1)
            act.wait_ge(parts_dve, mirrors(len(STEPS0) - 1))
            s_hi(0, 0)
            s_hi(0, 1)
            act.wait_ge(dinv_ready, 1)
            act.wait_ge(h0_ready, NT)
            for t in range(NT):
                nc.scalar.activation(G_hi[:, t, :], H0[:, t, :], ACT.Copy, scale=dinv[:, t:t + 1]).then_inc(g_hi_ready, 1)
                if t in (5, 9):
                    s_hi(0, 2 + (t == 9))

            def u_hi(m, j):
                act.wait_ge(ring_used, NQ * m + NQ)
                nc.scalar.activation(U[:, 0:QT, ds(m * P, P)], Y[j][:, :].rearrange("p (c n) -> p c n", c=QT), ACT.Copy,
                                     scale=half_dinv[:, ds(m, 1)]).then_inc(u_hi_ready, 1)

            act.wait_ge(hdinv_ready, 1)

            def weight_hi(n, t):
                if (n, t) == (0, 0):
                    act.wait_ge(w_in, 16 * 6)
                    act.wait_ge(lo_ready, NQ * (NT - 4))
                nc.scalar.activation(w_hi(n, t), w_tile(n, t), ACT.Copy).then_inc(w_hi_ready, 1)

            def bias_row_hi(n):
                act.wait_ge(bsum_step, DT * (n + 1))
                nc.scalar.activation(bias_hi(n), bias_sum(n), ACT.Copy).then_inc(bsum_hi_ready, 1)

            def phase1(m, j, extra=()):
                extra = list(extra)

                def more():
                    if extra:
                        f, *args = extra.pop(0)
                        f(*args)

                s_hi(m, 0)
                more()
                s_hi(m, 1)
                u_hi(m - 1, 1 - j)
                more()
                s_hi(m, 2)
                more()
                s_hi(m, 3)
                more()

            phase1(1, 1)
            with act.Fori(1, NT // 2 - 2) as i:
                for j in range(2):
                    phase1(2 * i + j, j)
            phase1(NT - 4, 0, [(weight_hi, 0, t) for t in range(DT)])
            phase1(NT - 3, 1, [(weight_hi, 1, t) for t in range(DT)])
            phase1(NT - 2, 0, [(bias_row_hi, 0), (bias_row_hi, 1)])
            phase1(NT - 1, 1)
            u_hi(NT - 1, 1)

            for a in range(DT):
                act.wait_ge(wprod_done, a + 1)
                nc.scalar.activation(M_w[:, 0, a, :], Z[a][:, :], ACT.Copy, scale=SCALE).then_inc(wprod_hi, 1)
            for a in range(DT):
                act.wait_ge(wprod_done, DT + a + 1)
                nc.scalar.activation(WvT[:, 0, a, :], Z[a][:, :], ACT.Copy).then_inc(wprod_hi, 1)

            def h_hi(m, j):
                act.wait_ge(h_T, m + 1)
                nc.scalar.activation(HT[:, 0:DT, ds(m * P, P)], Z[j][:, :].rearrange("p (a n) -> p a n", a=DT),
                                     ACT.Relu).then_inc(hT_hi, 1)

            def phase2(m, j):
                for q in range(1, NQ):
                    t_hi(m, RING2, q)
                if not isinstance(m, int) or m >= 1:
                    h_hi(m - 1, 1 - j)
                if not isinstance(m, int) or m < NT - 1:
                    t_hi(m + 1, RING2, 0)

            t_hi(0, RING2, 0)
            for m in range(2):
                phase2(m, m)
            with act.Fori(1, NT // 2 - 1) as i:
                for j in range(2):
                    phase2(2 * i + j, j)
            for m in range(NT - 2, NT):
                phase2(m, m % 2)

            def q_hi(g):
                for a in range(DT):
                    act.wait_ge(qt_done, DT * g + a + 1)
                    nc.scalar.activation(q_T[:, 0, a, :], TB[a % 2][:, :], ACT.Identity,
                                         bias=qbias[:, a:a + 1]).then_inc(qt_hi, 1)

            for t in range(NT):
                if t == 2:
                    h_hi(NT - 1, 1)
                if t == NT - 2:
                    q_hi(0)
                act.wait_ge(vsum_ready, t + 1)
                nc.scalar.activation(V[:, 0, t, :], x_out[:, t % 2, :], ACT.Copy).then_inc(v_hi_ready, 1)

            def exps(t, j):
                act.wait_ge(nmax_ready, t + 1)
                nc.scalar.activation(prob[j][:, :], prob[j][:, :], ACT.Exp, bias=nmax[:, j:j + 1],
                                     accum_out=rowsum[:, j:j + 1]).then_inc(prob_ready, 1)

            def relu(t, j):
                act.wait_ge(ring_used, NQ * t + RING3 + NQ)
                act.wait_ge(rinv_ready, t + 1)
                if not isinstance(t, int) or t >= 2:
                    act.wait_ge(out_stored[j], 8 * (t - j))
                nc.scalar.activation(x_out[:, j, :], Y[j][:, :], ACT.Relu,
                                     scale=rinv[:, j:j + 1]).then_inc(relu_ready, 1)

            def phase3(g, r, first_group, last_group):
                t, j = QT * g + r, r % 2
                if not (first_group and r == 0):
                    relu(t - 1, 1 - j)
                t_hi(t, RING3, 0)
                t_hi(t, RING3, 1)
                if r == QT - 2 and not last_group:
                    q_hi(g + 1)
                t_hi(t, RING3, 2)
                t_hi(t, RING3, 3)
                if not (last_group and r == QT - 1):
                    exps(t + 1, 1 - j)

            exps(0, 0)
            for r in range(QT):
                phase3(0, r, True, False)
            with act.Fori(1, QT - 1) as g:
                for r in range(QT):
                    phase3(g, r, False, False)
            for r in range(QT):
                phase3(QT - 1, r, False, True)
            relu(NT - 1, 1)

        @block.vector
        def _(dve):
            def s_lo(m, q):
                dve.wait_ge(hi_ready, NQ * m + q + 1)
                nc.vector.tensor_tensor(ring_lo[q % 2][:, :, :], S[:, QT * q:QT * q + QT, ds(m * P, P)],
                                        ring_hi[q % 2][:, :, :].bitcast(f32), ALU.subtract).then_inc(lo_ready, 1)

            def t_lo(m, ring0, q):
                dve.wait_ge(hi_ready, NQ * m + ring0 + q + 1)
                nc.vector.tensor_tensor(ring_lo[q % 2][:, :, :], TB[q % 2][:, :].rearrange("p (k n) -> p k n", k=QT),
                                        ring_hi[q % 2][:, :, :].bitcast(f32), ALU.subtract).then_inc(lo_ready, 1)

            nc.vector.memset(neg_half[:, :], -0.5).then_inc(half_ready, 1)
            nc.vector.memset(row_parts[:, :, :], 0.0).then_inc(parts_zero, 1)
            dve.wait_ge(parts_zero, 1)

            def mirror(n):
                r, b, c0_, c1_ = STEPS0[n]
                dve.wait_ge(mirror_done, mirror_steps(n))
                for c in range(c0_, below(r, c1_)):
                    nc.vector.tensor_scalar(S[:, c, r * P:(r + 1) * P], bank[2 * (n % 4)][:, (c - c0_) * P:(c - c0_ + 1) * P],
                                            1.0, None, ALU.mult, ALU.add,
                                            accum_out=row_parts[:, c, NQ + r:NQ + r + 1]).then_inc(parts_dve, 1)

            for n, (r, b, c0_, c1_) in enumerate(STEPS0):
                if b == 0 and 1 <= r < 5:
                    dve.wait_ge(x_in0[r - 1], 16)
                    for t in range(4 * (r - 1), 4 * (r - 1) + 4):
                        nc.vector.bn_stats(bn0[:, t, :], H0[:, t, :]).then_inc(bn0_ready, 1)
                dve.wait_ge(t0_done, n + 1)
                here = S[:, r, c0_ * P:c1_ * P]
                nc.vector.scalar_tensor_tensor(here, bank[2 * (n % 4) + 1][:, 0:(c1_ - c0_) * P], 1.0, here,
                                               ALU.mult, ALU.add, accum_out=row_parts[:, r, b:b + 1]).then_inc(s_added, 1)
                if n and by_dve(n - 1):
                    mirror(n - 1)
                if r == 5 and c1_ == r + 1:
                    dve.wait_ge(bn0_ready, NT)
                    for t in range(NT):
                        nc.vector.bn_aggr(mv0[:, t, :], bn0[:, t, :]).then_inc(mv0_ready, 1)
                    dve.wait_ge(mv0_ready, NT)
                    nc.vector.tensor_scalar(rstd0[:, :], mv0[:, :, 1], EPS, None, ALU.add).then_inc(var0_ready, 1)
                    dve.wait_ge(rstd0_ready, 1)
                    nc.vector.scalar_tensor_tensor(shift0[:, :], mv0[:, :, 0], -1.0, rstd0[:, :], ALU.mult, ALU.mult)\
                        .then_inc(shift0_ready, 1)

            mirror(len(STEPS0) - 1)
            dve.wait_ge(parts_dve, mirrors(len(STEPS0) - 1))
            dve.wait_ge(s_added, len(STEPS0))
            dve.wait_ge(parts_act, mirrors(len(STEPS0) - 2))
            nc.vector.tensor_reduce(deg[:, :], row_parts[:, :, :], AX, ALU.add).then_inc(deg_step, 1)
            dve.wait_ge(deg_step, 1)
            nc.vector.tensor_scalar(deg_pos[:, :], deg[:, :], 0.0, None, ALU.is_gt).then_inc(deg_step, 1)
            nc.vector.tensor_scalar(dinv[:, :], deg[:, :], 0.5, TINY, ALU.mult, ALU.max).then_inc(deg_step, 1)
            s_lo(0, 0)
            s_lo(0, 1)
            dve.wait_ge(dpow_ready, 1)
            nc.vector.tensor_tensor(dinv[:, :], deg[:, :], deg_pos[:, :], ALU.mult).then_inc(dinv_ready, 1)
            dve.wait_ge(dinv_ready, 1)
            nc.vector.tensor_scalar(half_dinv[:, :], dinv[:, :], 0.5, None, ALU.mult).then_inc(hdinv_ready, 1)

            for t in range(NT):
                dve.wait_ge(g_hi_ready, t + 1)
                nc.vector.scalar_tensor_tensor(G_lo[:, t, :], H0[:, t, :], dinv[:, t:t + 1], G_hi[:, t, :].bitcast(f32),
                                               ALU.mult, ALU.subtract).then_inc(g_ready, 1)
                if t in (5, 9):
                    s_lo(0, 2 + (t == 9))

            def u_lo(m, j):
                dve.wait_ge(u_hi_ready, m + 1)
                nc.vector.scalar_tensor_tensor(U[:, QT:2 * QT, ds(m * P, P)], Y[j][:, :].rearrange("p (c n) -> p c n", c=QT),
                                               half_dinv[:, ds(m, 1)], U[:, 0:QT, ds(m * P, P)].bitcast(f32),
                                               ALU.mult, ALU.subtract).then_inc(u_ready, 1)

            def bias_row(n, t):
                if (n, t) == (0, 0):
                    dve.wait_ge(bias_in, 48)
                    dve.wait_ge(w_in, 16 * 6)
                b_col = (bq_col, bk_col)[n][:, t:t + 1]
                if t == 0:
                    nc.vector.tensor_scalar(bias_sum(n), w_tile(1 - n, t), b_col, None, ALU.mult).then_inc(bsum_step, 1)
                else:
                    dve.wait_ge(bsum_step, DT * n + t)
                    nc.vector.scalar_tensor_tensor(bias_sum(n), w_tile(1 - n, t), b_col, bias_sum(n),
                                                   ALU.mult, ALU.add).then_inc(bsum_step, 1)

            def bias_row_lo(n):
                dve.wait_ge(bsum_hi_ready, n + 1)
                nc.vector.tensor_tensor(bias_lo(n), bias_sum(n), bias_hi(n).bitcast(f32),
                                        ALU.subtract).then_inc(bsum_lo_ready, 1)

            def weight_lo(n, t):
                dve.wait_ge(w_hi_ready, DT * n + t + 1)
                nc.vector.tensor_tensor(w_lo(n, t), w_tile(n, t), w_hi(n, t).bitcast(f32),
                                        ALU.subtract).then_inc(w_lo_ready, 1)

            def ones_and_bqk():
                nc.vector.memset(ones, 1.0).then_inc(ones_ready, 1)
                dve.wait_ge(ones_ready, 1)
                nc.vector.tensor_copy(ones_r, ones).then_inc(ones_ready, 1)
                nc.vector.scalar_tensor_tensor(bqk4[:, :], bq_col[:, :], 1.0, bk_col[:, :], ALU.mult, ALU.mult,
                                               accum_out=bqk[:, :]).then_inc(bqk_ready, 1)

            def phase1(m, j, extra=()):
                extra = list(extra)

                def more():
                    if extra:
                        f, *args = extra.pop(0)
                        f(*args)

                s_lo(m, 0)
                more()
                s_lo(m, 1)
                u_lo(m - 1, 1 - j)
                s_lo(m, 2)
                more()
                s_lo(m, 3)
                more()
                more()

            phase1(1, 1)
            with dve.Fori(1, NT // 2 - 2) as i:
                for j in range(2):
                    phase1(2 * i + j, j)
            phase1(NT - 4, 0, [(bias_row, 0, t) for t in range(DT)])
            phase1(NT - 3, 1, [(bias_row, 1, t) for t in range(DT)])
            phase1(NT - 2, 0, [(weight_lo, 0, t) for t in range(DT)])
            phase1(NT - 1, 1, [(weight_lo, 1, t) for t in range(DT)])
            bias_row_lo(0)
            bias_row_lo(1)
            ones_and_bqk()
            u_lo(NT - 1, 1)

            dve.wait_ge(wsmall_done, 1)
            for a in range(DT):
                blk = slice(a * P, (a + 1) * P)
                nc.vector.scalar_tensor_tensor(junk[:, blk], TB[0][:, blk], SCALE, ident[:, :], ALU.mult, ALU.mult,
                                               accum_out=qbias[:, a:a + 1]).then_inc(wsmall_ready, 1)
            nc.vector.tensor_scalar(wrow[:, :], TB[1][:, :], SCALE, None, ALU.mult).then_inc(wsmall_ready, 1)
            nc.vector.tensor_scalar(c0[:, :], Y[0][:, 0:1], SCALE, None, ALU.mult).then_inc(wsmall_ready, 1)
            for a in range(DT):
                dve.wait_ge(wprod_hi, a + 1)
                nc.vector.scalar_tensor_tensor(M_w[:, 1, a, :], Z[a][:, :], SCALE, M_w[:, 0, a, :].bitcast(f32),
                                               ALU.mult, ALU.subtract).then_inc(wprod_lo, 1)
            for a in range(DT):
                dve.wait_ge(wprod_hi, DT + a + 1)
                nc.vector.tensor_tensor(WvT[:, 1, a, :], Z[a][:, :], WvT[:, 0, a, :].bitcast(f32),
                                        ALU.subtract).then_inc(wprod_lo, 1)
            dve.wait_ge(wsmall_ready, DT + 2)

            def stats1(m, j):
                dve.wait_ge(ring_used, NQ * m + RING2 + NQ)
                if isinstance(m, int):
                    dve.wait_ge(xt_in[j], 16 * (m // 2 + 1))
                else:
                    dve.wait_ge(xt_in[j], 8 * (m - j) + 16)
                if not isinstance(m, int) or m >= 2:
                    dve.wait_ge(x1_stored[j], 8 * (m - j))
                nc.vector.tensor_tensor(x_out[:, j, :], Y[j][:, :], x_in[:, j, :], ALU.add)\
                    .then_inc(x1_ready, 1)
                dve.wait_ge(x1_ready, m + 1)
                nc.vector.bn_stats(bn[:, 6 * j:6 * j + 6], x_out[:, j, :]).then_inc(bn_ready, 1)
                dve.wait_ge(half_ready, 1)
                dve.wait_ge(bn_ready, m + 1)
                nc.vector.bn_aggr(mv[:, 2 * j:2 * j + 2], bn[:, 6 * j:6 * j + 6]).then_inc(mv_ready, 1)
                dve.wait_ge(mv_ready, m + 1)
                nc.vector.tensor_scalar(vareps[:, j:j + 1], mv[:, 2 * j + 1:2 * j + 2], EPS, None, ALU.add)\
                    .then_inc(var_ready, 1)

            def norm1(m, j):
                dve.wait_ge(rstd_ready, m + 1)
                if not isinstance(m, int) or m >= 2:
                    dve.wait_ge(h_T, m - 1)
                nc.vector.tensor_scalar(normed[:, j, :], x_out[:, j, :], mv[:, 2 * j:2 * j + 1], rstd[:, j:j + 1],
                                        ALU.subtract, ALU.mult).then_inc(norm_ready, 1)
                dve.wait_ge(norm_ready, m + 1)
                if not isinstance(m, int) or m >= 1:
                    dve.wait_ge(cdot_ready, m)
                nc.vector.scalar_tensor_tensor(junk[:, :], normed[:, j, :], 0.0, wrow[:, :], ALU.max, ALU.mult,
                                               accum_out=cbias[:, ds(m, 1)]).then_inc(cdot_ready, 1)

            def h_lo(m, j):
                dve.wait_ge(hT_hi, m + 1)
                nc.vector.scalar_tensor_tensor(HT[:, DT:2 * DT, ds(m * P, P)], Z[j][:, :].rearrange("p (a n) -> p a n", a=DT),
                                               0.0, HT[:, 0:DT, ds(m * P, P)].bitcast(f32),
                                               ALU.max, ALU.subtract).then_inc(hT_lo, 1)

            def phase2(m, j):
                later = not isinstance(m, int) or m >= 1
                t_lo(m, RING2, 1)
                if later:
                    stats1(m - 1, 1 - j)
                t_lo(m, RING2, 2)
                if later:
                    norm1(m - 1, 1 - j)
                t_lo(m, RING2, 3)
                if later:
                    h_lo(m - 1, 1 - j)
                if not isinstance(m, int) or m < NT - 1:
                    t_lo(m + 1, RING2, 0)

            t_lo(0, RING2, 0)
            for m in range(2):
                phase2(m, m)
            with dve.Fori(1, NT // 2 - 1) as i:
                for j in range(2):
                    phase2(2 * i + j, j)
            for m in range(NT - 2, NT):
                phase2(m, m % 2)
            stats1(NT - 1, 1)
            norm1(NT - 1, 1)
            dve.wait_ge(cdot_ready, NT)
            nc.vector.tensor_scalar(cbias[:, :], cbias[:, :], c0[:, 0:1], None, ALU.add).then_inc(cbias_ready, 1)

            def q_lo(g):
                for a in range(DT):
                    dve.wait_ge(qt_hi, DT * g + a + 1)
                    nc.vector.scalar_tensor_tensor(q_T[:, 1, a, :], TB[a % 2][:, :], qbias[:, a:a + 1],
                                                   q_T[:, 0, a, :].bitcast(f32), ALU.add, ALU.subtract).then_inc(qt_lo, 1)

            for j in range(2):
                dve.wait_ge(x1_stored[j], 16 * NT // 2)
            for t in range(NT):
                if t == 2:
                    h_lo(NT - 1, 1)
                if t == NT - 2:
                    q_lo(0)
                dve.wait_ge(v_done, t + 1)
                if t >= 2:
                    dve.wait_ge(v_ready, t - 1)
                nc.vector.tensor_tensor(x_out[:, t % 2, :], Y[t % 2][:, :], bv_row[:, :], ALU.add)\
                    .then_inc(vsum_ready, 1)
                dve.wait_ge(vsum_ready, t + 1)
                dve.wait_ge(v_hi_ready, t + 1)
                nc.vector.tensor_tensor(V[:, 1, t, :], x_out[:, t % 2, :], V[:, 0, t, :].bitcast(f32),
                                        ALU.subtract).then_inc(v_ready, 1)

            def score(t, j, n):
                dve.wait_ge(z_done, NQ * t + n + 1)
                if n == 0:
                    dve.wait_ge(adj_in, 16 * t + 16)
                    if not isinstance(t, int) or t >= 2:
                        dve.wait_ge(blocks_T, NQ * t + RING3 - RING2 - NQ)
                s = prob[j][:, n * D:(n + 1) * D]
                nc.vector.scalar_tensor_tensor(s, Z[n][:, :], cbias[:, ds(t, 1)], adj_row[:, n * D:(n + 1) * D],
                                               ALU.add, ALU.mult).then_inc(s_ready, 1)
                dve.wait_ge(s_ready, NQ * t + n + 1)
                if not (isinstance(t, int) and t == 0 and n == 0):
                    dve.wait_ge(masked_ready, NQ * t + n)
                nc.vector.tensor_scalar(junk[:, :], s, 0.0, MASKED, ALU.is_equal, ALU.mult).then_inc(mask_ready, 1)
                dve.wait_ge(half_ready, 1)
                dve.wait_ge(mask_ready, NQ * t + n + 1)
                nc.vector.tensor_tensor_reduce(s, s, junk[:, :], 1.0, -3.0e38, ALU.add, ALU.max,
                                               accum_out=mx4[:, NQ * j + n:NQ * j + n + 1]).then_inc(masked_ready, 1)

            def row_max(t, j):
                dve.wait_ge(masked_ready, NQ * t + NQ)
                nc.vector.tensor_reduce(nmax[:, j:j + 1], mx4[:, NQ * j:NQ * j + NQ], AX, ALU.max, negate=True)\
                    .then_inc(nmax_ready, 1)

            def finish(t, j):
                dve.wait_ge(relu_ready, t + 1)
                if isinstance(t, int):
                    dve.wait_ge(x1_in[j], 16 * (t // 2 + 1))
                else:
                    dve.wait_ge(x1_in[j], 8 * (t - j) + 16)
                nc.vector.tensor_tensor(x_out[:, j, :], x_out[:, j, :], x_in[:, j, :], ALU.add).then_inc(out_ready, 1)

            def phase3(g, r, first_group, last_group):
                t, j = QT * g + r, r % 2
                final = last_group and r == QT - 1
                dve.wait_ge(prob_ready, t + 1)
                nc.vector.reciprocal(rinv[:, j:j + 1], rowsum[:, j:j + 1]).then_inc(rinv_ready, 1)
                if not (first_group and r == 0):
                    finish(t - 1, 1 - j)
                if not final:
                    for n in range(NQ - 1):
                        score(t + 1, 1 - j, n)
                t_lo(t, RING3, 0)
                t_lo(t, RING3, 1)
                if not final:
                    score(t + 1, 1 - j, NQ - 1)
                    row_max(t + 1, 1 - j)
                if r == QT - 2 and not last_group:
                    q_lo(g + 1)
                t_lo(t, RING3, 2)
                t_lo(t, RING3, 3)

            dve.wait_ge(cbias_ready, 1)
            for n in range(NQ):
                score(0, 0, n)
            row_max(0, 0)
            for r in range(QT):
                phase3(0, r, True, False)
            with dve.Fori(1, QT - 1) as g:
                for r in range(QT):
                    phase3(g, r, False, False)
            for r in range(QT):
                phase3(QT - 1, r, False, True)
            finish(NT - 1, 1)

        @block.gpsimd
        def _(pool):
            nc.gpsimd.memset(ident[:, :], 0.0).then_inc(ident_step, 1)
            pool.wait_ge(ident_step, 1)
            nc.gpsimd.affine_select(out=ident[:, :], in_=ident[:, :], compare_op=ALU.not_equal, fill=1.0, base=0,
                                    pattern=[[-1, P]], channel_multiplier=1).then_inc(ident_ready, 1)
            pool.wait_ge(ident_ready, 1)
            nc.gpsimd.tensor_scalar(ident2[:, :], ident[:, :], 2.0, None, ALU.mult).then_inc(ident2_ready, 1)
            pool.wait_ge(half_ready, 1)
            pool.wait_ge(var0_ready, 1)
            nc.gpsimd.tensor_tensor(rstd0[:, :], rstd0[:, :], neg_half[:, :], ALU.pow).then_inc(rstd0_ready, 1)
            pool.wait_ge(deg_step, 3)
            nc.gpsimd.tensor_tensor(deg[:, :], dinv[:, :], neg_half[:, :], ALU.pow).then_inc(dpow_ready, 1)

            def rstds(m, j):
                pool.wait_ge(var_ready, m + 1)
                nc.gpsimd.tensor_tensor(rstd[:, j:j + 1], vareps[:, j:j + 1], neg_half[:, 0:1], ALU.pow)\
                    .then_inc(rstd_ready, 1)

            with pool.Fori(0, NT // 2) as i:
                for j in range(2):
                    rstds(2 * i + j, j)


_INS = ["x", "adj", "L1_gnn_W_q", "L1_gnn_b_q", "L1_gnn_W_k", "L1_gnn_b_k", "L1_gnn_W_v", "L1_gnn_b_v"]


def kernel(**inputs):
    import numpy as _np
    import concourse.bacc as _bacc
    from concourse import mybir as _mybir
    from concourse.bass_utils import run_bass_kernel_spmd as _run

    nc = _bacc.Bacc("TRN2", target_bir_lowering=False, num_devices=1)
    arrays, args = {}, []
    for name in _INS:
        a = _np.ascontiguousarray(inputs[name])
        arrays[f"in_{name}"] = a
        args.append(nc.dram_tensor(f"in_{name}", a.shape, _mybir.dt.from_np(a.dtype), kind="ExternalInput").ap())
    out = nc.dram_tensor("x2", (N, D), _mybir.dt.float32, kind="ExternalOutput").ap()
    build(nc, *args, out)
    r = _run(nc, [arrays], core_ids=[0])
    return r.results[0]["x2"]
```

```python
import concourse.bass as bass
from concourse import mybir
from concourse.alu_op_type import AluOpType as ALU
from contextlib import ExitStack

N = 2048
D = 512
P = 128
NT = N // P
DT = D // P
QT = 4
NQ = NT // QT
EPS = 1e-5
MASKED = -10000.0
SCALE = 1.0 / float(D) ** 0.5
TINY = 1.17549435e-38


def build(nc, x, adj, w_q, b_q, w_k, b_k, w_v, b_v, out):
    f32, f32r = mybir.dt.float32, mybir.dt.float32r
    ACT = mybir.ActivationFunctionType
    AX = mybir.AxisListType.X
    ds = bass.ds

    x_t = x.rearrange("(t p) d -> p t d", p=P)
    wq_t = w_q.rearrange("(t p) d -> p t d", p=P)
    wk_t = w_k.rearrange("(t p) d -> p t d", p=P)
    wv_t = w_v.rearrange("(t p) d -> p t d", p=P)
    x1_dram = nc.dram_tensor("x1_scratch", [N, D], f32).ap()

    BASE = (nc.sbuf_base + 31) // 32 * 32
    KB = 1024
    REG_S = BASE
    REG_G = REG_S + 128 * KB
    REG_R = REG_G + 64 * KB

    def at(name, shape, dt, offset):
        return nc.alloc_sbuf_tensor_at(name, shape, dt, offset=offset)

    S = at("S", [P, NT, N], f32, REG_S)
    U = at("U", [P, NT // 2, N], f32r, REG_S)
    W = at("W", [P, NT // 2, N], f32, REG_S + 64 * KB)
    HT = at("HT", [P, 2 * DT, N], f32r, REG_S + 64 * KB)
    V = at("V", [P, 2, NT, D], f32r, REG_S)
    H0 = at("H0", [P, NT, D], f32, REG_G + 32 * KB)
    G_hi = at("G_hi", [P, NT, D], f32r, REG_G)
    G_lo = at("G_lo", [P, NT, D], f32r, REG_G + 32 * KB)
    A_row = at("A_row", [P, 2, N], f32, REG_G)
    M_w = at("M_w", [P, 2, DT, D], f32r, REG_G + 16 * KB)
    WvT = at("WvT", [P, 2, DT, D], f32r, REG_G + 32 * KB)
    x_in = at("x_in", [P, 2, D], f32, REG_G + 48 * KB)
    x_out = at("x_out", [P, 2, D], f32, REG_G + 52 * KB)
    normed = at("normed", [P, 2, D], f32, REG_G + 56 * KB)
    adj_row = at("adj_row", [P, N], f32, REG_G + 32 * KB)
    prob = [at("prob0", [P, N], f32, REG_G + 40 * KB), at("prob1", [P, N], f32, REG_G + 56 * KB)]
    q_T = at("q_T", [P, 2, DT, D], f32r, REG_G)
    ring_hi = [at(f"ring_hi{b}", [P, QT, P], f32r, REG_R + 2 * KB * b) for b in range(2)]
    ring_lo = [at(f"ring_lo{b}", [P, QT, P], f32r, REG_R + 4 * KB + 2 * KB * b) for b in range(2)]
    PARTS = NQ + NT
    row_parts = at("row_parts", [P, NT, PARTS], f32, REG_G + 30 * KB)
    bn0 = at("bn0", [P, NT, 6], f32, REG_G + 29 * KB)
    mv0 = at("mv0", [P, NT, 2], f32, REG_G + 28 * KB)
    ident2 = at("ident2", [P, P], f32, REG_G + 27 * KB)
    ident = at("ident", [P, P], f32, REG_R + 8 * KB)
    wrow = at("wrow", [P, D], f32, REG_R + 8 * KB + 512)
    bv_row = at("bv_row", [P, D], f32, REG_R + 10 * KB + 512)
    junk = at("junk", [P, D], f32, REG_R + 12 * KB + 512)
    small = REG_R + 14 * KB + 512
    cols = {}
    for name, n in (("neg_half", NT), ("deg", NT), ("deg_pos", NT), ("deg_min", NT), ("dpow", NT),
                    ("half_dinv", NT), ("rstd0", NT), ("pos_rstd", NT), ("g_scale", NT), ("cbias", NT), ("bq_col", DT), ("bk_col", DT),
                    ("qbias", DT), ("c0", 1), ("bqk", 1), ("bqk4", DT), ("bn", 12), ("mv", 4), ("vareps", 2), ("rstd", 2),
                    ("mx4", 8), ("nmax", 2), ("rowsum", 2), ("rinv", 2)):
        cols[name] = at(name, [P, n], f32, small)
        small += (4 * n + 31) // 32 * 32
    assert small <= nc.sbuf_usable_end, (small, nc.sbuf_usable_end)
    neg_half, deg, deg_pos, deg_min, dpow = (cols[k] for k in ("neg_half", "deg", "deg_pos", "deg_min", "dpow"))
    half_dinv, pos_rstd, g_scale = (cols[k] for k in ("half_dinv", "pos_rstd", "g_scale"))
    rstd0, cbias, bq_col, bk_col = (cols[k] for k in ("rstd0", "cbias", "bq_col", "bk_col"))
    qbias, c0, bn, mv, vareps, rstd = (cols[k] for k in ("qbias", "c0", "bn", "mv", "vareps", "rstd"))
    bqk, bqk4 = cols["bqk"], cols["bqk4"]
    mx4, nmax, rowsum, rinv = (cols[k] for k in ("mx4", "nmax", "rowsum", "rinv"))

    W_r = at("W_r", [P, NT // 2, N], f32r, REG_S + 64 * KB)

    def w_place(tensor, n, t):
        return tensor[:, 2 * n + t // 2, (t % 2) * D:(t % 2 + 1) * D]

    def w_tile(n, t):
        return w_place(W, n, t)

    def w_lo(n, t):
        return w_place(W_r, n, t)

    def w_hi(n, t):
        return W_r[:, DT * n + t, 2 * D:3 * D]

    def bias_sum(n):
        return W[:, 6, n * D:(n + 1) * D]

    def bias_lo(n):
        return W_r[:, 6, n * D:(n + 1) * D]

    def bias_hi(n):
        return W_r[:, 7, n * D:(n + 1) * D]

    ones_r = W_r[:, 0, 3 * D:3 * D + P]
    ones = W[:, 1, 3 * D:3 * D + P]

    ctx = ExitStack()
    with ctx:
        bank = [ctx.enter_context(nc.psum_tensor(f"bank{i}", [P, D], f32)) for i in range(8)]
        Z, TB, Y = bank[0:4], bank[4:6], bank[6:8]

        def sem(name):
            return ctx.enter_context(nc.semaphore(name))

        a_in = [sem(f"a_in{r}") for r in range(NT)]
        x_in0 = [sem(f"x_in0_{k}") for k in range(4)]
        bias_in = sem("bias_in")
        w_in = sem("w_in")
        arow_in = [sem(f"arow_in{i}") for i in range(2)]
        xt_in = [sem(f"xt_in{i}") for i in range(2)]
        x1_stored = [sem(f"x1_stored{i}") for i in range(2)]
        adj_in = sem("adj_in")
        adj1_in = sem("adj1_in")
        x1_in = [sem(f"x1_in{i}") for i in range(2)]
        out_stored = [sem(f"out_stored{i}") for i in range(2)]
        ident_step, ident_ready, half_ready = sem("ident_step"), sem("ident_ready"), sem("half_ready")
        t0_done, s_added, parts_act, mirror_done = (sem(k) for k in ("t0_done", "s_added", "parts_act", "mirror_done"))
        parts_zero, parts_dve, ident2_ready = sem("parts_zero"), sem("parts_dve"), sem("ident2_ready")
        bn0_ready, mv0_ready, var0_ready, rstd0_ready = (
            sem(k) for k in ("bn0_ready", "mv0_ready", "var0_ready", "rstd0_ready"))
        h0_ready, deg_ready, deg_min_ready, deg_pos_ready, dpow_ready, pos_rstd_ready, g_scale_ready, hdinv_ready = (
            sem(k) for k in ("h0_ready", "deg_ready", "deg_min_ready", "deg_pos_ready", "dpow_ready", "pos_rstd_ready",
                             "g_scale_ready", "hdinv_ready"))
        g_hi_ready, g_ready = sem("g_hi_ready"), sem("g_ready")
        hi_ready, lo_ready, ring_used = sem("hi_ready"), sem("lo_ready"), sem("ring_used")
        blocks_T = sem("blocks_T")
        u_hi_ready, u_ready = sem("u_hi_ready"), sem("u_ready")
        w_hi_ready, w_lo_ready, ones_ready = sem("w_hi_ready"), sem("w_lo_ready"), sem("ones_ready")
        bsum_step, bsum_hi_ready, bsum_lo_ready, bqk_ready = (
            sem(k) for k in ("bsum_step", "bsum_hi_ready", "bsum_lo_ready", "bqk_ready"))
        wsmall_done, wsmall_ready = sem("wsmall_done"), sem("wsmall_ready")
        wprod_done, wprod_hi, wprod_lo = sem("wprod_done"), sem("wprod_hi"), sem("wprod_lo")
        x1_ready, bn_ready, mv_ready, var_ready, rstd_ready, norm_ready = (
            sem(k) for k in ("x1_ready", "bn_ready", "mv_ready", "var_ready", "rstd_ready", "norm_ready"))
        cdot_ready, cbias_ready = sem("cdot_ready"), sem("cbias_ready")
        h_T, hT_hi, hT_lo = sem("h_T"), sem("hT_hi"), sem("hT_lo")
        v_done = sem("v_done")
        vsum_ready, v_hi_ready, v_ready = sem("vsum_ready"), sem("v_hi_ready"), sem("v_ready")
        qt_done, qt_hi, qt_lo = sem("qt_done"), sem("qt_hi"), sem("qt_lo")
        z_done, s_ready, mask_ready, masked_ready = sem("z_done"), sem("s_ready"), sem("mask_ready"), sem("masked_ready")
        nmax_ready, prob_ready = sem("nmax_ready"), sem("prob_ready")
        rinv_ready, relu_ready, out_ready = sem("rinv_ready"), sem("relu_ready"), sem("out_ready")

        RING2, RING3 = NT * NQ, 2 * NT * NQ

        def batches(r):
            return [(c, min(c + QT, r + 1)) for c in range(0, r + 1, QT)]

        STEPS0 = [(r, b, c0_, c1_) for r in range(NT) for b, (c0_, c1_) in enumerate(batches(r))]

        def below(r, c1_):
            return min(c1_, r)

        def by_dve(n):
            return STEPS0[n][0] >= DVE_SHARE and STEPS0[n][1] % 2 == 1

        def mirrors(n):
            return sum(below(r, c1_) - c0_ for k, (r, b, c0_, c1_) in enumerate(STEPS0[:n + 1]) if by_dve(k) == by_dve(n))

        def mirror_steps(n):
            return sum(below(r, c1_) > c0_ for r, b, c0_, c1_ in STEPS0[:n + 1])

        DVE_SHARE = 13
        STAGE_AT = (7, 10, 13)
        AHEAD = 3

        def three(pe_out, hi_l, lo_l, hi_r, lo_r, first, last):
            nc.tensor.matmul(pe_out, hi_l, hi_r, start=first, stop=False)
            nc.tensor.matmul(pe_out, hi_l, lo_r, start=False, stop=False)
            return nc.tensor.matmul(pe_out, lo_l, hi_r, start=False, stop=last)

        block = ctx.enter_context(nc.Block())

        @block.sync
        def _(sp):
            for r in range(NT):
                sp.dma_start(S[:, r, :], adj[r * P:(r + 1) * P, :]).then_inc(a_in[r], 16)
                if r < 4:
                    sp.dma_start(H0[:, 4 * r:4 * r + 4, :], x_t[:, 4 * r:4 * r + 4, :]).then_inc(x_in0[r], 16)
            with nc.allow_non_contiguous_dma(reason="512 bias values, one a partition and tile"):
                sp.dma_start(bq_col[:, :], b_q.rearrange("(t p) -> p t", p=P)).then_inc(bias_in, 16)
                sp.dma_start(bk_col[:, :], b_k.rearrange("(t p) -> p t", p=P)).then_inc(bias_in, 16)
            sp.dma_start(bv_row[:, :], b_v.partition_broadcast(P)).then_inc(bias_in, 16)
            sp.wait_ge(lo_ready, NT // 2 * NQ)
            for n, w_dram in enumerate((wq_t, wk_t, wv_t)):
                for h in range(2):
                    sp.dma_start(W[:, 2 * n + h, 0:2 * D].rearrange("p (t d) -> p t d", t=2),
                                 w_dram[:, 2 * h:2 * h + 2, :]).then_inc(w_in, 16)
            sp.wait_ge(ring_used, RING2)

            def rows_in(m, j):
                sp.dma_start(A_row[:, j, :], adj[ds(m * P, P), :]).then_inc(arow_in[j], 16)
                sp.dma_start(x_in[:, j, :], x[ds(m * P, P), :]).then_inc(xt_in[j], 16)

            def x1_store(m, j):
                sp.wait_ge(x1_ready, m + 1)
                sp.dma_start(x1_dram[ds(m * P, P), :], x_out[:, j, :]).then_inc(x1_stored[j], 16)

            for m in range(2):
                rows_in(m, m)
            with sp.Fori(0, NT // 2 - 1) as i:
                for j in range(2):
                    m = 2 * i + j
                    sp.wait_ge(x1_ready, m + 1)
                    sp.wait_ge(blocks_T, NQ * m + NQ)
                    rows_in(m + 2, j)
                    x1_store(m, j)
            for m in range(NT - 2, NT):
                x1_store(m, m % 2)
            for j in range(2):
                sp.wait_ge(x1_stored[j], 16 * NT // 2)

            def adj_load(i):
                sp.dma_start(adj_row[:, :], adj[ds(i * P, P), :]).then_inc(adj_in, 16)

            def x1_load(i, j):
                sp.dma_start(x_in[:, j, :], x1_dram[ds(i * P, P), :]).then_inc(x1_in[j], 16)

            def out_store(i, j):
                sp.wait_ge(out_ready, i + 1)
                sp.dma_start(out[ds(i * P, P), :], x_out[:, j, :]).then_inc(out_stored[j], 16)

            x1_load(0, 0)
            x1_load(1, 1)
            sp.wait_ge(v_done, NT)
            adj_load(0)
            sp.dma_start(prob[1][:, :], adj[P:2 * P, :]).then_inc(adj1_in, 16)
            with sp.Fori(0, NT // 2 - 1) as i:
                for j in range(2):
                    t = 2 * i + j
                    sp.wait_ge(s_ready, NQ * t + 2 * NQ)
                    adj_load(t + 2)
                    out_store(t, j)
                    x1_load(t + 2, j)
            for t in range(NT - 2, NT):
                out_store(t, t % 2)
            for j in range(2):
                sp.wait_ge(out_stored[j], 16 * NT // 2)

        @block.tensor
        def _(pe):
            pe.wait_ge(ident_ready, 1)
            def mirror(n):
                r, b, c0_, c1_ = STEPS0[n]
                if below(r, c1_) == c0_:
                    return
                pe.wait_ge(s_added, n + 1)
                if n >= 4 and mirrors(n - 4):
                    pe.wait_ge(parts_dve if by_dve(n - 4) else parts_act, mirrors(n - 4))
                for c in range(c0_, below(r, c1_)):
                    last = nc.tensor.transpose(bank[2 * (n % 4)][:, (c - c0_) * P:(c - c0_ + 1) * P],
                                               S[:, r, c * P:(c + 1) * P], ident[:, :])
                last.then_inc(mirror_done, 1)

            for n, (r, b, c0_, c1_) in enumerate(STEPS0):
                if b == 0 and r >= 1:
                    pe.wait_ge(a_in[r - 1], 16)
                if n >= 4:
                    pe.wait_ge(s_added, n - 3)
                low = bank[2 * (n % 4) + 1]
                for c in range(c0_, below(r, c1_)):
                    last = nc.tensor.transpose(low[:, (c - c0_) * P:(c - c0_ + 1) * P],
                                               S[:, c, r * P:(r + 1) * P], ident[:, :])
                if c1_ == r + 1:
                    if r == 0:
                        pe.wait_ge(ident2_ready, 1)
                    pe.wait_ge(a_in[r], 16)
                    diag = low[:, (r - c0_) * P:(r - c0_ + 1) * P]
                    nc.tensor.matmul(diag, S[:, r, r * P:(r + 1) * P], ident[:, :], start=True, stop=False)
                    last = nc.tensor.matmul(diag, ident2[:, :], ident[:, :], start=False, stop=True)
                last.then_inc(t0_done, 1)
                if n >= AHEAD:
                    mirror(n - AHEAD)
            for n in range(len(STEPS0) - AHEAD, len(STEPS0)):
                mirror(n)
            pe.wait_ge(s_added, len(STEPS0))

            def phase1(m, j):
                pe.wait_ge(u_ready, m - 1)
                for q in range(NQ):
                    pe.wait_ge(lo_ready, NQ * m + q + 1)
                    for k in range(QT):
                        t = QT * q + k
                        last = three(Y[j][:, :], ring_hi[q % 2][:, k, :], ring_lo[q % 2][:, k, :],
                                     G_hi[:, t, :], G_lo[:, t, :], t == 0, t == NT - 1)
                    last.then_inc(ring_used, 1)

            for n in range(2 * NQ):
                q, m = n // 2, n % 2
                pe.wait_ge(lo_ready, n + 1)
                for k in range(QT):
                    t = QT * q + k
                    pe.wait_ge(g_ready, t + 1)
                    last = three(Y[m][:, :], ring_hi[m][:, k, :], ring_lo[m][:, k, :],
                                 G_hi[:, t, :], G_lo[:, t, :], t == 0, t == NT - 1)
                last.then_inc(ring_used, 1)
            with pe.Fori(1, NT // 2) as i:
                for j in range(2):
                    phase1(2 * i + j, j)

            pe.wait_ge(w_lo_ready, 2 * DT)
            def m_product(a):
                rows = slice(a * P, (a + 1) * P)
                for e in range(DT):
                    last = three(Z[a][:, :], w_hi(0, e)[:, rows], w_lo(0, e)[:, rows], w_hi(1, e), w_lo(1, e),
                                 e == 0, e == DT - 1)
                last.then_inc(wprod_done, 1)

            m_product(0)
            pe.wait_ge(bsum_lo_ready, 2)
            pe.wait_ge(ones_ready, 2)
            for n in range(2):
                nc.tensor.matmul(TB[n][:, :], ones_r, bias_hi(n), start=True, stop=False)
                nc.tensor.matmul(TB[n][:, :], ones_r, bias_lo(n), start=False, stop=True)
            pe.wait_ge(u_ready, NT - 1)
            pe.wait_ge(bqk_ready, 1)
            nc.tensor.matmul(Y[0][:, 0:1], ones, bqk[:, :], start=True, stop=True).then_inc(wsmall_done, 1)
            m_product(1)
            m_product(2)

            def transposes(q, j):
                for k in range(QT):
                    last = nc.tensor.transpose(TB[q % 2][:, k * P:(k + 1) * P],
                                               A_row[:, j, (QT * q + k) * P:(QT * q + k + 1) * P], ident[:, :])
                last.then_inc(blocks_T, 1)

            def transpose_h(m, j):
                pe.wait_ge(norm_ready, m + 1)
                if not isinstance(m, int) or m >= 2:
                    pe.wait_ge(hT_lo, m - 1)
                else:
                    pe.wait_ge(wprod_lo, 2 * DT)
                for a in range(DT):
                    last = nc.tensor.transpose(Z[j][:, a * P:(a + 1) * P], normed[:, j, a * P:(a + 1) * P], ident[:, :])
                last.then_inc(h_T, 1)

            def phase2(m, j):
                if not isinstance(m, int) or m >= 2:
                    pe.wait_ge(x1_ready, m - 1)
                for q in range(NQ):
                    if q < NQ - 1:
                        transposes(q + 1, j)
                    elif not isinstance(m, int) or m < NT - 1:
                        pe.wait_ge(arow_in[1 - j], arrived(m, j))
                        transposes(0, 1 - j)
                    if q == 2 and (not isinstance(m, int) or m >= 1):
                        transpose_h(m - 1, 1 - j)
                    pe.wait_ge(lo_ready, NQ * m + RING2 + q + 1)
                    for k in range(QT):
                        t = QT * q + k
                        u = U[:, :, t * P:(t + 1) * P]
                        last = three(Y[j][:, :].rearrange("p (c n) -> p c n", c=QT), ring_hi[q % 2][:, k, :], ring_lo[q % 2][:, k, :],
                                     u[:, 0:QT, :], u[:, QT:2 * QT, :], t == 0, t == NT - 1)
                    last.then_inc(ring_used, 1)

            def arrived(m, j):
                return 16 * ((m + 1) // 2 + 1) if isinstance(m, int) else 8 * (m - j) + 16 * j + 16

            pe.wait_ge(wsmall_ready, DT + 2)
            pe.wait_ge(arow_in[0], 16)
            transposes(0, 0)
            m_product(3)
            for a in range(DT):
                pe.wait_ge(wprod_lo, a + 1)
                for e in range(DT):
                    last = nc.tensor.transpose(Z[a][:, e * P:(e + 1) * P], w_tile(2, e)[:, a * P:(a + 1) * P], ident[:, :])
                last.then_inc(wprod_done, 1)
            pe.wait_ge(u_ready, NT)
            for m in range(2):
                phase2(m, m)
            with pe.Fori(1, NT // 2 - 1) as i:
                for j in range(2):
                    phase2(2 * i + j, j)
            for m in range(NT - 2, NT):
                phase2(m, m % 2)

            def v_tile(t):
                pe.wait_ge(hT_lo, t + 1)
                if t < 2:
                    pe.wait_ge(x1_ready, NT - 1 + t)
                else:
                    pe.wait_ge(vsum_ready, t - 1)
                for a in range(DT):
                    rows = slice(t * P, (t + 1) * P)
                    last = three(Y[t % 2][:, :], HT[:, a, rows], HT[:, DT + a, rows],
                                 WvT[:, 0, a, :], WvT[:, 1, a, :], a == 0, a == DT - 1)
                last.then_inc(v_done, 1)

            def q_group(g):
                for a in range(DT):
                    if a >= 2:
                        pe.wait_ge(qt_lo, DT * g + a - 1)
                    for d in range(DT):
                        cols_g = ds(g * D, D)
                        last = three(TB[a % 2][:, :], M_w[:, 0, d, a * P:(a + 1) * P], M_w[:, 1, d, a * P:(a + 1) * P],
                                     HT[:, d, cols_g], HT[:, DT + d, cols_g], d == 0, d == DT - 1)
                    last.then_inc(qt_done, 1)

            def z_bank(t, r, n):
                pe.wait_ge(s_ready, NQ * t + n - (NQ - 1)) if not isinstance(t, int) or t >= 1 else None
                for d in range(DT):
                    last = three(Z[n][:, :], q_T[:, 0, d, r * P:(r + 1) * P], q_T[:, 1, d, r * P:(r + 1) * P],
                                 HT[:, d, n * D:(n + 1) * D], HT[:, DT + d, n * D:(n + 1) * D], d == 0, d == DT - 1)
                last.then_inc(z_done, 1)

            def transpose_p(j, q):
                for k in range(QT):
                    last = nc.tensor.transpose(TB[q % 2][:, k * P:(k + 1) * P],
                                               prob[j][:, (QT * q + k) * P:(QT * q + k + 1) * P], ident[:, :])
                last.then_inc(blocks_T, 1)

            def pv(t, j, q):
                for k in range(QT):
                    c = QT * q + k
                    last = three(Y[j][:, :], ring_hi[q % 2][:, k, :], ring_lo[q % 2][:, k, :],
                                 V[:, 0, c, :], V[:, 1, c, :], c == 0, c == NT - 1)
                last.then_inc(ring_used, 1)

            def phase3(g, r, first_group, last_group):
                t, j = QT * g + r, r % 2
                final = last_group and r == QT - 1
                if not final:
                    if r == QT - 1:
                        pe.wait_ge(qt_lo, DT * g + 2 * DT)
                    for n in range(NQ - 1):
                        z_bank(t + 1, (r + 1) % QT, n)
                pe.wait_ge(prob_ready, t + 1)
                if not (first_group and r == 0):
                    pe.wait_ge(lo_ready, NQ * t + RING3)
                transpose_p(j, 0)
                transpose_p(j, 1)
                if not final:
                    z_bank(t + 1, (r + 1) % QT, NQ - 1)
                q_next = r == QT - 2 and not last_group
                if q_next:
                    pe.wait_ge(lo_ready, NQ * t + RING3 + 2)
                    q_group(g + 1)
                if not (first_group and r < 2):
                    pe.wait_ge(relu_ready, t - 1)
                for q in range(NQ):
                    pe.wait_ge(lo_ready, NQ * t + RING3 + q + 1)
                    if q < NQ - 2:
                        if q_next:
                            pe.wait_ge(qt_lo, DT * g + 2 * DT - 1 + q)
                        transpose_p(j, q + 2)
                    pv(t, j, q)

            for t in range(NT):
                if t == 2:
                    transpose_h(NT - 1, 1)
                if t == NT - 2:
                    q_group(0)
                v_tile(t)
            pe.wait_ge(qt_lo, DT)
            for n in range(NQ):
                z_bank(0, 0, n)
            pe.wait_ge(v_ready, NT)
            for r in range(QT):
                phase3(0, r, True, False)
            with pe.Fori(1, QT - 1) as g:
                for r in range(QT):
                    phase3(g, r, False, False)
            for r in range(QT):
                phase3(QT - 1, r, False, True)

        @block.scalar
        def _(act):
            def s_hi(m, q):
                act.wait_ge(ring_used, NQ * m + q - 1)
                nc.scalar.activation(ring_hi[q % 2][:, :, :], S[:, QT * q:QT * q + QT, ds(m * P, P)],
                                     ACT.Copy).then_inc(hi_ready, 1)

            def s_hi_01(n):
                q, m = n // 2, n % 2
                if n >= 2:
                    act.wait_ge(ring_used, n - 1)
                nc.scalar.activation(ring_hi[m][:, :, :], S[:, QT * q:QT * q + QT, m * P:(m + 1) * P],
                                     ACT.Copy).then_inc(hi_ready, 1)

            def t_hi(m, ring0, q):
                act.wait_ge(blocks_T, NQ * m + ring0 - RING2 + q + 1)
                act.wait_ge(ring_used, NQ * m + ring0 + q - 1)
                nc.scalar.activation(ring_hi[q % 2][:, :, :], TB[q % 2][:, :].rearrange("p (k n) -> p k n", k=QT),
                                     ACT.Copy).then_inc(hi_ready, 1)

            act.wait_ge(parts_zero, 1)
            for n, (r, b, c0_, c1_) in enumerate(STEPS0):
                if not by_dve(n) and below(r, c1_) > c0_:
                    act.wait_ge(mirror_done, mirror_steps(n))
                    for c in range(c0_, below(r, c1_)):
                        nc.scalar.activation(S[:, c, r * P:(r + 1) * P],
                                             bank[2 * (n % 4)][:, (c - c0_) * P:(c - c0_ + 1) * P], ACT.Copy,
                                             accum_out=row_parts[:, c, NQ + r:NQ + r + 1]).then_inc(parts_act, 1)
            act.wait_ge(parts_dve, mirrors(len(STEPS0) - 1))
            s_hi_01(0)
            s_hi_01(1)
            act.wait_ge(h0_ready, NT)
            for t in range(NT):
                if t % 4 == 0:
                    act.wait_ge(g_scale_ready, t // 4 + 1)
                nc.scalar.activation(G_hi[:, t, :], H0[:, t, :], ACT.Copy, scale=g_scale[:, t:t + 1]).then_inc(g_hi_ready, 1)
                if t in STAGE_AT:
                    s_hi_01(2 + STAGE_AT.index(t))

            def u_hi(m, j):
                act.wait_ge(ring_used, 2 * NQ - 1 if isinstance(m, int) and m == 0 else NQ * m + NQ)
                nc.scalar.activation(U[:, 0:QT, ds(m * P, P)], Y[j][:, :].rearrange("p (c n) -> p c n", c=QT), ACT.Copy,
                                     scale=half_dinv[:, ds(m, 1)]).then_inc(u_hi_ready, 1)

            act.wait_ge(hdinv_ready, 1)

            def weight_hi(n, t):
                if (n, t) == (0, 0):
                    act.wait_ge(w_in, 16 * 6)
                    act.wait_ge(lo_ready, NQ * (NT - 4))
                nc.scalar.activation(w_hi(n, t), w_tile(n, t), ACT.Copy).then_inc(w_hi_ready, 1)

            def bias_row_hi(n):
                act.wait_ge(bsum_step, DT * (n + 1))
                nc.scalar.activation(bias_hi(n), bias_sum(n), ACT.Copy).then_inc(bsum_hi_ready, 1)

            def phase1(m, j, extra=()):
                extra = list(extra)

                def more():
                    if extra:
                        f, *args = extra.pop(0)
                        f(*args)

                s_hi(m, 0)
                more()
                s_hi(m, 1)
                u_hi(m - 1, 1 - j)
                more()
                s_hi(m, 2)
                more()
                s_hi(m, 3)
                more()

            for n in range(2 + len(STAGE_AT), 2 * NQ):
                s_hi_01(n)
            u_hi(0, 0)
            with act.Fori(1, NT // 2 - 2) as i:
                for j in range(2):
                    phase1(2 * i + j, j)
            phase1(NT - 4, 0, [(weight_hi, 0, t) for t in range(DT)])
            phase1(NT - 3, 1, [(weight_hi, 1, t) for t in range(DT)])
            phase1(NT - 2, 0, [(bias_row_hi, 0), (bias_row_hi, 1)])
            phase1(NT - 1, 1)
            u_hi(NT - 1, 1)

            def h_hi(m, j):
                act.wait_ge(h_T, m + 1)
                nc.scalar.activation(HT[:, 0:DT, ds(m * P, P)], Z[j][:, :].rearrange("p (a n) -> p a n", a=DT),
                                     ACT.Relu).then_inc(hT_hi, 1)

            def phase2(m, j):
                for q in range(1, NQ):
                    t_hi(m, RING2, q)
                if not isinstance(m, int) or m >= 1:
                    h_hi(m - 1, 1 - j)
                if not isinstance(m, int) or m < NT - 1:
                    t_hi(m + 1, RING2, 0)

            for a in range(DT):
                act.wait_ge(wprod_done, a + 1)
                nc.scalar.activation(M_w[:, 0, a, :], Z[a][:, :], ACT.Copy, scale=SCALE).then_inc(wprod_hi, 1)
                if a == DT - 2:
                    t_hi(0, RING2, 0)
            for a in range(DT):
                act.wait_ge(wprod_done, DT + a + 1)
                nc.scalar.activation(WvT[:, 0, a, :], Z[a][:, :], ACT.Copy).then_inc(wprod_hi, 1)
            for m in range(2):
                phase2(m, m)
            with act.Fori(1, NT // 2 - 1) as i:
                for j in range(2):
                    phase2(2 * i + j, j)
            for m in range(NT - 2, NT):
                phase2(m, m % 2)

            def q_hi(g):
                for a in range(DT):
                    act.wait_ge(qt_done, DT * g + a + 1)
                    nc.scalar.activation(q_T[:, 0, a, :], TB[a % 2][:, :], ACT.Identity,
                                         bias=qbias[:, a:a + 1]).then_inc(qt_hi, 1)

            for t in range(NT):
                if t == 2:
                    h_hi(NT - 1, 1)
                if t == NT - 2:
                    q_hi(0)
                act.wait_ge(vsum_ready, t + 1)
                nc.scalar.activation(V[:, 0, t, :], x_out[:, t % 2, :], ACT.Copy).then_inc(v_hi_ready, 1)

            def exps(t, j):
                act.wait_ge(nmax_ready, t + 1)
                nc.scalar.activation(prob[j][:, :], prob[j][:, :], ACT.Exp, bias=nmax[:, j:j + 1],
                                     accum_out=rowsum[:, j:j + 1]).then_inc(prob_ready, 1)

            def relu(t, j):
                act.wait_ge(ring_used, NQ * t + RING3 + NQ)
                act.wait_ge(rinv_ready, t + 1)
                if not isinstance(t, int) or t >= 2:
                    act.wait_ge(out_stored[j], 8 * (t - j))
                nc.scalar.activation(x_out[:, j, :], Y[j][:, :], ACT.Relu,
                                     scale=rinv[:, j:j + 1]).then_inc(relu_ready, 1)

            def phase3(g, r, first_group, last_group):
                t, j = QT * g + r, r % 2
                final = last_group and r == QT - 1
                if not (first_group and r == 0) and not final:
                    relu(t - 1, 1 - j)
                t_hi(t, RING3, 0)
                t_hi(t, RING3, 1)
                if final:
                    relu(t - 1, 1 - j)
                if r == QT - 2 and not last_group:
                    q_hi(g + 1)
                t_hi(t, RING3, 2)
                t_hi(t, RING3, 3)
                if not final:
                    exps(t + 1, 1 - j)

            exps(0, 0)
            for r in range(QT):
                phase3(0, r, True, False)
            with act.Fori(1, QT - 1) as g:
                for r in range(QT):
                    phase3(g, r, False, False)
            for r in range(QT):
                phase3(QT - 1, r, False, True)
            relu(NT - 1, 1)

        @block.vector
        def _(dve):
            def s_lo(m, q):
                dve.wait_ge(hi_ready, NQ * m + q + 1)
                nc.vector.tensor_tensor(ring_lo[q % 2][:, :, :], S[:, QT * q:QT * q + QT, ds(m * P, P)],
                                        ring_hi[q % 2][:, :, :].bitcast(f32), ALU.subtract).then_inc(lo_ready, 1)

            def s_lo_01(n):
                q, m = n // 2, n % 2
                dve.wait_ge(hi_ready, n + 1)
                nc.vector.tensor_tensor(ring_lo[m][:, :, :], S[:, QT * q:QT * q + QT, m * P:(m + 1) * P],
                                        ring_hi[m][:, :, :].bitcast(f32), ALU.subtract).then_inc(lo_ready, 1)

            def t_lo(m, ring0, q):
                dve.wait_ge(hi_ready, NQ * m + ring0 + q + 1)
                nc.vector.tensor_tensor(ring_lo[q % 2][:, :, :], TB[q % 2][:, :].rearrange("p (k n) -> p k n", k=QT),
                                        ring_hi[q % 2][:, :, :].bitcast(f32), ALU.subtract).then_inc(lo_ready, 1)

            nc.vector.memset(neg_half[:, :], -0.5).then_inc(half_ready, 1)
            nc.vector.memset(row_parts[:, :, :], 0.0).then_inc(parts_zero, 1)
            dve.wait_ge(parts_zero, 1)

            def mirror(n):
                r, b, c0_, c1_ = STEPS0[n]
                dve.wait_ge(mirror_done, mirror_steps(n))
                for c in range(c0_, below(r, c1_)):
                    nc.vector.tensor_scalar(S[:, c, r * P:(r + 1) * P], bank[2 * (n % 4)][:, (c - c0_) * P:(c - c0_ + 1) * P],
                                            1.0, None, ALU.mult, ALU.add,
                                            accum_out=row_parts[:, c, NQ + r:NQ + r + 1]).then_inc(parts_dve, 1)

            for n, (r, b, c0_, c1_) in enumerate(STEPS0):
                if b == 0 and 1 <= r < 5:
                    tiles = range(4 * (r - 1), 4 * r)
                    dve.wait_ge(x_in0[r - 1], 16)
                    for t in tiles:
                        nc.vector.bn_stats(bn0[:, t, :], H0[:, t, :]).then_inc(bn0_ready, 1)
                    dve.wait_ge(bn0_ready, 4 * r)
                    for t in tiles:
                        nc.vector.bn_aggr(mv0[:, t, :], bn0[:, t, :]).then_inc(mv0_ready, 1)
                    dve.wait_ge(mv0_ready, 4 * r)
                    for t in tiles:
                        nc.vector.tensor_scalar(H0[:, t, :], H0[:, t, :], mv0[:, t, 0:1], 0.0,
                                                ALU.subtract, ALU.max).then_inc(h0_ready, 1)
                    if r == 4:
                        nc.vector.tensor_scalar(rstd0[:, :], mv0[:, :, 1], EPS, None, ALU.add).then_inc(var0_ready, 1)
                if b == 0:
                    dve.wait_ge(a_in[r], 16)
                dve.wait_ge(t0_done, n + 1)
                here = S[:, r, c0_ * P:c1_ * P]
                nc.vector.scalar_tensor_tensor(here, bank[2 * (n % 4) + 1][:, 0:(c1_ - c0_) * P], 1.0, here,
                                               ALU.mult, ALU.add, accum_out=row_parts[:, r, b:b + 1]).then_inc(s_added, 1)
                if n >= AHEAD and by_dve(n - AHEAD):
                    mirror(n - AHEAD)

            for n in range(len(STEPS0) - AHEAD, len(STEPS0)):
                if by_dve(n):
                    mirror(n)
            LAST0 = len(STEPS0) - 1
            dve.wait_ge(parts_dve, mirrors(LAST0))
            dve.wait_ge(s_added, len(STEPS0))
            dve.wait_ge(parts_act, mirrors(LAST0 - 1))
            nc.vector.tensor_reduce(deg[:, :], row_parts[:, :, :], AX, ALU.add).then_inc(deg_ready, 1)
            dve.wait_ge(deg_ready, 1)
            nc.vector.tensor_scalar(deg_min[:, :], deg[:, :], 0.5, TINY, ALU.mult, ALU.max).then_inc(deg_min_ready, 1)
            nc.vector.tensor_scalar(deg_pos[:, :], deg[:, :], 0.0, None, ALU.is_gt).then_inc(deg_pos_ready, 1)
            dve.wait_ge(rstd0_ready, 1)
            dve.wait_ge(deg_pos_ready, 1)
            nc.vector.tensor_tensor(pos_rstd[:, :], deg_pos[:, :], rstd0[:, :], ALU.mult).then_inc(pos_rstd_ready, 1)

            def g_scales(k):
                four = slice(4 * k, 4 * k + 4)
                dve.wait_ge(dpow_ready, k + 1)
                nc.vector.tensor_tensor(g_scale[:, four], dpow[:, four], pos_rstd[:, four], ALU.mult)\
                    .then_inc(g_scale_ready, 1)

            s_lo_01(0)
            dve.wait_ge(pos_rstd_ready, 1)
            g_scales(0)
            s_lo_01(1)

            for t in range(NT):
                dve.wait_ge(g_hi_ready, t + 1)
                nc.vector.scalar_tensor_tensor(G_lo[:, t, :], H0[:, t, :], g_scale[:, t:t + 1], G_hi[:, t, :].bitcast(f32),
                                               ALU.mult, ALU.subtract).then_inc(g_ready, 1)
                if t in (0, 2, 4):
                    g_scales(t // 2 + 1)
                if t in STAGE_AT:
                    s_lo_01(2 + STAGE_AT.index(t))
            nc.vector.scalar_tensor_tensor(half_dinv[:, :], dpow[:, :], 0.5, deg_pos[:, :], ALU.mult, ALU.mult)\
                .then_inc(hdinv_ready, 1)

            def u_lo(m, j):
                dve.wait_ge(u_hi_ready, m + 1)
                nc.vector.scalar_tensor_tensor(U[:, QT:2 * QT, ds(m * P, P)], Y[j][:, :].rearrange("p (c n) -> p c n", c=QT),
                                               half_dinv[:, ds(m, 1)], U[:, 0:QT, ds(m * P, P)].bitcast(f32),
                                               ALU.mult, ALU.subtract).then_inc(u_ready, 1)

            def bias_row(n, t):
                if (n, t) == (0, 0):
                    dve.wait_ge(bias_in, 48)
                    dve.wait_ge(w_in, 16 * 6)
                b_col = (bq_col, bk_col)[n][:, t:t + 1]
                if t == 0:
                    nc.vector.tensor_scalar(bias_sum(n), w_tile(1 - n, t), b_col, None, ALU.mult).then_inc(bsum_step, 1)
                else:
                    dve.wait_ge(bsum_step, DT * n + t)
                    nc.vector.scalar_tensor_tensor(bias_sum(n), w_tile(1 - n, t), b_col, bias_sum(n),
                                                   ALU.mult, ALU.add).then_inc(bsum_step, 1)

            def bias_row_lo(n):
                dve.wait_ge(bsum_hi_ready, n + 1)
                nc.vector.tensor_tensor(bias_lo(n), bias_sum(n), bias_hi(n).bitcast(f32),
                                        ALU.subtract).then_inc(bsum_lo_ready, 1)

            def weight_lo(n, t):
                dve.wait_ge(w_hi_ready, DT * n + t + 1)
                nc.vector.tensor_tensor(w_lo(n, t), w_tile(n, t), w_hi(n, t).bitcast(f32),
                                        ALU.subtract).then_inc(w_lo_ready, 1)

            def ones_and_bqk():
                nc.vector.memset(ones, 1.0).then_inc(ones_ready, 1)
                dve.wait_ge(ones_ready, 1)
                nc.vector.tensor_copy(ones_r, ones).then_inc(ones_ready, 1)
                nc.vector.scalar_tensor_tensor(bqk4[:, :], bq_col[:, :], 1.0, bk_col[:, :], ALU.mult, ALU.mult,
                                               accum_out=bqk[:, :]).then_inc(bqk_ready, 1)

            def phase1(m, j, extra=()):
                extra = list(extra)

                def more():
                    if extra:
                        f, *args = extra.pop(0)
                        f(*args)

                s_lo(m, 0)
                more()
                s_lo(m, 1)
                u_lo(m - 1, 1 - j)
                s_lo(m, 2)
                more()
                s_lo(m, 3)
                more()
                more()

            for n in range(2 + len(STAGE_AT), 2 * NQ):
                s_lo_01(n)
            u_lo(0, 0)
            with dve.Fori(1, NT // 2 - 2) as i:
                for j in range(2):
                    phase1(2 * i + j, j)
            phase1(NT - 4, 0, [(bias_row, 0, t) for t in range(DT)])
            phase1(NT - 3, 1, [(bias_row, 1, t) for t in range(DT)])
            phase1(NT - 2, 0, [(weight_lo, 0, t) for t in range(DT)])
            phase1(NT - 1, 1, [(weight_lo, 1, t) for t in range(DT)])
            bias_row_lo(0)
            bias_row_lo(1)
            ones_and_bqk()
            u_lo(NT - 1, 1)

            dve.wait_ge(wsmall_done, 1)
            for a in range(DT):
                blk = slice(a * P, (a + 1) * P)
                nc.vector.scalar_tensor_tensor(junk[:, blk], TB[0][:, blk], SCALE, ident[:, :], ALU.mult, ALU.mult,
                                               accum_out=qbias[:, a:a + 1]).then_inc(wsmall_ready, 1)
            nc.vector.tensor_scalar(wrow[:, :], TB[1][:, :], SCALE, None, ALU.mult).then_inc(wsmall_ready, 1)
            nc.vector.tensor_scalar(c0[:, :], Y[0][:, 0:1], SCALE, None, ALU.mult).then_inc(wsmall_ready, 1)

            def stats1(m, j):
                dve.wait_ge(ring_used, NQ * m + RING2 + NQ)
                if isinstance(m, int):
                    dve.wait_ge(xt_in[j], 16 * (m // 2 + 1))
                else:
                    dve.wait_ge(xt_in[j], 8 * (m - j) + 16)
                if not isinstance(m, int) or m >= 2:
                    dve.wait_ge(x1_stored[j], 8 * (m - j))
                nc.vector.tensor_tensor(x_out[:, j, :], Y[j][:, :], x_in[:, j, :], ALU.add)\
                    .then_inc(x1_ready, 1)
                dve.wait_ge(x1_ready, m + 1)
                nc.vector.bn_stats(bn[:, 6 * j:6 * j + 6], x_out[:, j, :]).then_inc(bn_ready, 1)
                dve.wait_ge(half_ready, 1)
                dve.wait_ge(bn_ready, m + 1)
                nc.vector.bn_aggr(mv[:, 2 * j:2 * j + 2], bn[:, 6 * j:6 * j + 6]).then_inc(mv_ready, 1)
                dve.wait_ge(mv_ready, m + 1)
                nc.vector.tensor_scalar(vareps[:, j:j + 1], mv[:, 2 * j + 1:2 * j + 2], EPS, None, ALU.add)\
                    .then_inc(var_ready, 1)

            def norm1(m, j):
                dve.wait_ge(rstd_ready, m + 1)
                if not isinstance(m, int) or m >= 2:
                    dve.wait_ge(h_T, m - 1)
                nc.vector.tensor_scalar(normed[:, j, :], x_out[:, j, :], mv[:, 2 * j:2 * j + 1], rstd[:, j:j + 1],
                                        ALU.subtract, ALU.mult).then_inc(norm_ready, 1)
                dve.wait_ge(norm_ready, m + 1)
                if not isinstance(m, int) or m >= 1:
                    dve.wait_ge(cdot_ready, m)
                nc.vector.scalar_tensor_tensor(junk[:, :], normed[:, j, :], 0.0, wrow[:, :], ALU.max, ALU.mult,
                                               accum_out=cbias[:, ds(m, 1)]).then_inc(cdot_ready, 1)

            def h_lo(m, j):
                dve.wait_ge(hT_hi, m + 1)
                nc.vector.scalar_tensor_tensor(HT[:, DT:2 * DT, ds(m * P, P)], Z[j][:, :].rearrange("p (a n) -> p a n", a=DT),
                                               0.0, HT[:, 0:DT, ds(m * P, P)].bitcast(f32),
                                               ALU.max, ALU.subtract).then_inc(hT_lo, 1)

            def phase2(m, j):
                later = not isinstance(m, int) or m >= 1
                t_lo(m, RING2, 1)
                if later:
                    stats1(m - 1, 1 - j)
                t_lo(m, RING2, 2)
                if later:
                    norm1(m - 1, 1 - j)
                t_lo(m, RING2, 3)
                if later:
                    h_lo(m - 1, 1 - j)
                if not isinstance(m, int) or m < NT - 1:
                    t_lo(m + 1, RING2, 0)

            for a in range(DT):
                dve.wait_ge(wprod_hi, a + 1)
                nc.vector.scalar_tensor_tensor(M_w[:, 1, a, :], Z[a][:, :], SCALE, M_w[:, 0, a, :].bitcast(f32),
                                               ALU.mult, ALU.subtract).then_inc(wprod_lo, 1)
                if a == DT - 2:
                    t_lo(0, RING2, 0)
            for a in range(DT):
                dve.wait_ge(wprod_hi, DT + a + 1)
                nc.vector.tensor_tensor(WvT[:, 1, a, :], Z[a][:, :], WvT[:, 0, a, :].bitcast(f32),
                                        ALU.subtract).then_inc(wprod_lo, 1)
            dve.wait_ge(wsmall_ready, DT + 2)
            for m in range(2):
                phase2(m, m)
            with dve.Fori(1, NT // 2 - 1) as i:
                for j in range(2):
                    phase2(2 * i + j, j)
            for m in range(NT - 2, NT):
                phase2(m, m % 2)
            stats1(NT - 1, 1)
            norm1(NT - 1, 1)
            dve.wait_ge(cdot_ready, NT)
            nc.vector.tensor_scalar(cbias[:, :], cbias[:, :], c0[:, 0:1], None, ALU.add).then_inc(cbias_ready, 1)

            def q_lo(g):
                for a in range(DT):
                    dve.wait_ge(qt_hi, DT * g + a + 1)
                    nc.vector.scalar_tensor_tensor(q_T[:, 1, a, :], TB[a % 2][:, :], qbias[:, a:a + 1],
                                                   q_T[:, 0, a, :].bitcast(f32), ALU.add, ALU.subtract).then_inc(qt_lo, 1)

            for j in range(2):
                dve.wait_ge(x1_stored[j], 16 * NT // 2)
            for t in range(NT):
                if t == 2:
                    h_lo(NT - 1, 1)
                if t == NT - 2:
                    q_lo(0)
                dve.wait_ge(v_done, t + 1)
                if t >= 2:
                    dve.wait_ge(v_ready, t - 1)
                nc.vector.tensor_tensor(x_out[:, t % 2, :], Y[t % 2][:, :], bv_row[:, :], ALU.add)\
                    .then_inc(vsum_ready, 1)
                dve.wait_ge(vsum_ready, t + 1)
                dve.wait_ge(v_hi_ready, t + 1)
                nc.vector.tensor_tensor(V[:, 1, t, :], x_out[:, t % 2, :], V[:, 0, t, :].bitcast(f32),
                                        ALU.subtract).then_inc(v_ready, 1)

            def score(t, j, n):
                dve.wait_ge(z_done, NQ * t + n + 1)
                if n == 0:
                    if isinstance(t, int) and t < 2:
                        dve.wait_ge((adj_in, adj1_in)[t], 16)
                    else:
                        dve.wait_ge(adj_in, 16 * t)
                    if not isinstance(t, int) or t >= 2:
                        dve.wait_ge(blocks_T, NQ * t + RING3 - RING2 - NQ)
                s = prob[j][:, n * D:(n + 1) * D]
                adj_part = s if isinstance(t, int) and t == 1 else adj_row[:, n * D:(n + 1) * D]
                nc.vector.scalar_tensor_tensor(s, Z[n][:, :], cbias[:, ds(t, 1)], adj_part,
                                               ALU.add, ALU.mult).then_inc(s_ready, 1)
                dve.wait_ge(s_ready, NQ * t + n + 1)
                if not (isinstance(t, int) and t == 0 and n == 0):
                    dve.wait_ge(masked_ready, NQ * t + n)
                nc.vector.tensor_scalar(junk[:, :], s, 0.0, MASKED, ALU.is_equal, ALU.mult).then_inc(mask_ready, 1)
                dve.wait_ge(half_ready, 1)
                dve.wait_ge(mask_ready, NQ * t + n + 1)
                nc.vector.tensor_tensor_reduce(s, s, junk[:, :], 1.0, -3.0e38, ALU.add, ALU.max,
                                               accum_out=mx4[:, NQ * j + n:NQ * j + n + 1]).then_inc(masked_ready, 1)

            def row_max(t, j):
                dve.wait_ge(masked_ready, NQ * t + NQ)
                nc.vector.tensor_reduce(nmax[:, j:j + 1], mx4[:, NQ * j:NQ * j + NQ], AX, ALU.max, negate=True)\
                    .then_inc(nmax_ready, 1)

            def finish(t, j):
                dve.wait_ge(relu_ready, t + 1)
                if isinstance(t, int):
                    dve.wait_ge(x1_in[j], 16 * (t // 2 + 1))
                else:
                    dve.wait_ge(x1_in[j], 8 * (t - j) + 16)
                nc.vector.tensor_tensor(x_out[:, j, :], x_out[:, j, :], x_in[:, j, :], ALU.add).then_inc(out_ready, 1)

            def phase3(g, r, first_group, last_group):
                t, j = QT * g + r, r % 2
                final = last_group and r == QT - 1
                if not (first_group and r == 0) and not final:
                    finish(t - 1, 1 - j)
                if not final:
                    for n in range(NQ - 1):
                        score(t + 1, 1 - j, n)
                t_lo(t, RING3, 0)
                t_lo(t, RING3, 1)
                dve.wait_ge(prob_ready, t + 1)
                nc.vector.reciprocal(rinv[:, j:j + 1], rowsum[:, j:j + 1]).then_inc(rinv_ready, 1)
                if final:
                    finish(t - 1, 1 - j)
                else:
                    score(t + 1, 1 - j, NQ - 1)
                    row_max(t + 1, 1 - j)
                if r == QT - 2 and not last_group:
                    q_lo(g + 1)
                t_lo(t, RING3, 2)
                t_lo(t, RING3, 3)

            dve.wait_ge(cbias_ready, 1)
            for n in range(NQ):
                score(0, 0, n)
            row_max(0, 0)
            for r in range(QT):
                phase3(0, r, True, False)
            with dve.Fori(1, QT - 1) as g:
                for r in range(QT):
                    phase3(g, r, False, False)
            for r in range(QT):
                phase3(QT - 1, r, False, True)
            finish(NT - 1, 1)

        @block.gpsimd
        def _(pool):
            nc.gpsimd.memset(ident[:, :], 0.0).then_inc(ident_step, 1)
            pool.wait_ge(ident_step, 1)
            nc.gpsimd.affine_select(out=ident[:, :], in_=ident[:, :], compare_op=ALU.not_equal, fill=1.0, base=0,
                                    pattern=[[-1, P]], channel_multiplier=1).then_inc(ident_ready, 1)
            pool.wait_ge(ident_ready, 1)
            nc.gpsimd.tensor_scalar(ident2[:, :], ident[:, :], 2.0, None, ALU.mult).then_inc(ident2_ready, 1)
            pool.wait_ge(half_ready, 1)
            pool.wait_ge(var0_ready, 1)
            nc.gpsimd.tensor_tensor(rstd0[:, :], rstd0[:, :], neg_half[:, :], ALU.pow).then_inc(rstd0_ready, 1)
            pool.wait_ge(deg_min_ready, 1)
            for k in range(4):
                four = slice(4 * k, 4 * k + 4)
                nc.gpsimd.tensor_tensor(dpow[:, four], deg_min[:, four], neg_half[:, four], ALU.pow).then_inc(dpow_ready, 1)

            def rstds(m, j):
                pool.wait_ge(var_ready, m + 1)
                nc.gpsimd.tensor_tensor(rstd[:, j:j + 1], vareps[:, j:j + 1], neg_half[:, 0:1], ALU.pow)\
                    .then_inc(rstd_ready, 1)

            with pool.Fori(0, NT // 2) as i:
                for j in range(2):
                    rstds(2 * i + j, j)


_INS = ["x", "adj", "L1_gnn_W_q", "L1_gnn_b_q", "L1_gnn_W_k", "L1_gnn_b_k", "L1_gnn_W_v", "L1_gnn_b_v"]


def kernel(**inputs):
    import numpy as _np
    import concourse.bacc as _bacc
    from concourse import mybir as _mybir
    from concourse.bass_utils import run_bass_kernel_spmd as _run

    nc = _bacc.Bacc("TRN2", target_bir_lowering=False, num_devices=1)
    arrays, args = {}, []
    for name in _INS:
        a = _np.ascontiguousarray(inputs[name])
        arrays[f"in_{name}"] = a
        args.append(nc.dram_tensor(f"in_{name}", a.shape, _mybir.dt.from_np(a.dtype), kind="ExternalInput").ap())
    out = nc.dram_tensor("x2", (N, D), _mybir.dt.float32, kind="ExternalOutput").ap()
    build(nc, *args, out)
    r = _run(nc, [arrays], core_ids=[0])
    return r.results[0]["x2"]
```
